# Optimizing a Trainium2 kernel written in Bass

```python
import numpy as np
import jax
import jax.numpy as jnp

def _softmax(x, axis=-1):
    return jax.nn.softmax(x, axis=axis)

def _gelu(x):
    return jax.nn.gelu(x, approximate=True)

def _silu(x):
    return jax.nn.silu(x)

def _sigmoid(x):
    return jax.nn.sigmoid(x)

def _layernorm(x, axis=-1, eps=1e-05):
    m = jnp.mean(x, axis=axis, keepdims=True)
    v = jnp.var(x, axis=axis, keepdims=True)
    return (x - m) / jnp.sqrt(v + eps)

def _scatter_add(tgt, idx, src, axis=0):
    return tgt.at[idx].add(src)

def _segment_sum(src, seg, n):
    return jax.ops.segment_sum(src, seg, n)
kernel_name = 'mk_adaln_ffn_d1_seqx_r4_63ffed'

def setup_inputs(seed: int=0):
    np.random.seed(seed)
    _w = jnp.asarray

    def _rec_inputs():
        import jax
        import jax.numpy as jnp
        _rk = jax.random.key(seed)
        x = -0.0003929 + 0.9999 * jax.random.normal(jax.random.fold_in(_rk, 1), (32, 64, 1024), jnp.float32)
        _lenS = 64 - jax.random.randint(jax.random.fold_in(_rk, 7), (32,), 0, max(1, 64 // 4) + 1, jnp.int32)
        _lenS2 = 64 - jax.random.randint(jax.random.fold_in(_rk, 8), (32,), 0, max(1, 64 // 4) + 1, jnp.int32)
        itok_B_8_3872 = jax.random.randint(jax.random.fold_in(_rk, 11), (32,), 8, 3873, jnp.int32)
        return (x, itok_B_8_3872)
    x, itok_B_8_3872 = _rec_inputs()

    def _L0_cond_setup():
        import math
        import jax, jax.numpy as jnp
        import numpy as np
        H, N, B, L = (64, 64, 16, 1024)
        DT_MIN, DT_MAX = (0.001, 0.1)

        def _get_kernel(log_dt, C, log_A_real, A_imag, length):
            Cc = C[..., 0] + 1j * C[..., 1]
            dt = jnp.exp(log_dt)
            A = -jnp.exp(log_A_real) + 1j * A_imag
            dtA = A * dt[:, None]
            P = dtA[:, :, None] * jnp.arange(length, dtype=jnp.float32)
            Cs = Cc * (jnp.exp(dtA) - 1.0) / A
            K = 2.0 * jnp.einsum('hn,hnl->hl', Cs, jnp.exp(P)).real
            return K
        key = jax.random.key(seed)
        ks = jax.random.split(key, 6)
        u = jax.random.normal(ks[0], (B, H, L), dtype=jnp.float32)
        length = jax.random.randint(ks[1], (B,), 0, L)
        log_dt = jax.random.uniform(ks[2], (H,), dtype=jnp.float32) * (math.log(DT_MAX) - math.log(DT_MIN)) + math.log(DT_MIN)
        C = jax.random.normal(ks[3], (H, N, 2), dtype=jnp.float32)
        log_A_real = jnp.log(0.5 * jnp.ones((H, N), dtype=jnp.float32))
        A_imag = math.pi * jnp.broadcast_to(jnp.arange(N, dtype=jnp.float32), (H, N))
        D = jax.random.normal(ks[4], (H,), dtype=jnp.float32)
        return {'u': u, 'length': length, 'log_dt': log_dt, 'C': C, 'log_A_real': log_A_real, 'A_imag': A_imag, 'D': D}
    _L0_cond_all = _L0_cond_setup()
    _L0_cond_in = {k: v for k, v in _L0_cond_all.items() if k in ('log_dt', 'C', 'log_A_real', 'A_imag', 'D')}
    del _L0_cond_all

    def _L0_ffn_setup():
        import jax, jax.numpy as jnp
        import numpy as np
        RANKS = (8, 16, 32, 64)
        TOPK = 1
        SCALING = 1.0 / 4
        key = jax.random.key(seed)
        ks = jax.random.split(key, 7)
        D_IN, D_OUT, MAX_R, N_RANKS = (1024, 1024, 64, len(RANKS))
        B_, S_ = (4, 512)
        return {'hidden_states': jax.random.normal(ks[0], (B_, S_, D_IN), jnp.float32), 'W': jax.random.normal(ks[1], (D_OUT, D_IN), jnp.float32) * 0.02, 'b': jax.random.normal(ks[2], (D_OUT,), jnp.float32) * 0.02, 'A': jax.random.normal(ks[3], (MAX_R, D_IN), jnp.float32) * 0.02, 'B': jnp.zeros((D_OUT, MAX_R), jnp.float32) + jax.random.normal(ks[4], (D_OUT, MAX_R), jnp.float32) * 0.02, 'gate_w': jax.random.normal(ks[5], (N_RANKS, D_IN), jnp.float32) * 0.02, 'gate_b': jax.random.normal(ks[6], (N_RANKS,), jnp.float32) * 0.02}
    _L0_ffn_all = _L0_ffn_setup()
    _L0_ffn_in = {k: v for k, v in _L0_ffn_all.items() if k in ('W', 'b', 'A', 'B', 'gate_w', 'gate_b')}
    del _L0_ffn_all
    return {'x': x, 'itok_B_8_3872': itok_B_8_3872, 'L0_cond_log_dt': _L0_cond_in['log_dt'], 'L0_cond_C': _L0_cond_in['C'], 'L0_cond_log_A_real': _L0_cond_in['log_A_real'], 'L0_cond_A_imag': _L0_cond_in['A_imag'], 'L0_cond_D': _L0_cond_in['D'], 'L0_ffn_W': _L0_ffn_in['W'], 'L0_ffn_b': _L0_ffn_in['b'], 'L0_ffn_A': _L0_ffn_in['A'], 'L0_ffn_B': _L0_ffn_in['B'], 'L0_ffn_gate_w': _L0_ffn_in['gate_w'], 'L0_ffn_gate_b': _L0_ffn_in['gate_b']}

def reference(x, itok_B_8_3872, L0_cond_log_dt, L0_cond_C, L0_cond_log_A_real, L0_cond_A_imag, L0_cond_D, L0_ffn_W, L0_ffn_b, L0_ffn_A, L0_ffn_B, L0_ffn_gate_w, L0_ffn_gate_b):
    import jax
    import jax.numpy as jnp

    def _L0_cond_ref(u, length, log_dt, C, log_A_real, A_imag, D):
        import math
        import jax, jax.numpy as jnp
        import numpy as np
        H, N, B, L = (64, 64, 16, 1024)
        DT_MIN, DT_MAX = (0.001, 0.1)

        def _get_kernel(log_dt, C, log_A_real, A_imag, length):
            Cc = C[..., 0] + 1j * C[..., 1]
            dt = jnp.exp(log_dt)
            A = -jnp.exp(log_A_real) + 1j * A_imag
            dtA = A * dt[:, None]
            P = dtA[:, :, None] * jnp.arange(length, dtype=jnp.float32)
            Cs = Cc * (jnp.exp(dtA) - 1.0) / A
            K = 2.0 * jnp.einsum('hn,hnl->hl', Cs, jnp.exp(P)).real
            return K
        Bq, Hq, Lq = u.shape
        mask = (jnp.arange(Lq) < length[:, None]).astype(u.dtype)
        u_m = u * mask[:, None, :]
        kernel = _get_kernel(log_dt, C, log_A_real, A_imag, Lq)
        n = 2 * Lq
        k_f = jnp.fft.rfft(kernel, n=n)
        u_f = jnp.fft.rfft(u_m, n=n)
        y = jnp.fft.irfft(u_f * k_f, n=n)[..., :Lq]
        y = y + u_m * D[:, None]
        return y * mask[:, None, :]

    def _L0_ffn_ref(hidden_states, W, b, A, B, gate_w, gate_b):
        import jax, jax.numpy as jnp
        import numpy as np
        RANKS = (8, 16, 32, 64)
        TOPK = 1
        SCALING = 1.0 / 4
        bsz, seq, d_in = hidden_states.shape
        out = jnp.einsum('bsd,od->bso', hidden_states, W) + b
        x = hidden_states.reshape(-1, d_in)
        scores = x @ gate_w.T + gate_b
        probs = jax.nn.softmax(scores, axis=-1)
        routing_weights, selected = jax.lax.top_k(probs, TOPK)
        routing_weights = routing_weights / jnp.sum(routing_weights, axis=-1, keepdims=True)
        lora_outputs = jnp.stack([x @ A[:r, :].T @ B[:, :r].T for r in RANKS], axis=1)
        sel = jnp.take_along_axis(lora_outputs, selected[:, :, None], axis=1)
        final = jnp.sum(sel * routing_weights[:, :, None], axis=1)
        return out + final.reshape(bsz, seq, -1)
    x = x + _L0_ffn_ref(_L0_cond_ref(x, itok_B_8_3872, L0_cond_log_dt, L0_cond_C, L0_cond_log_A_real, L0_cond_A_imag, L0_cond_D), L0_ffn_W, L0_ffn_b, L0_ffn_A, L0_ffn_B, L0_ffn_gate_w, L0_ffn_gate_b)
    return x

_drawn_inputs = setup_inputs


def setup_inputs(seed=0):
    import zlib

    import numpy as np

    out = dict(_drawn_inputs(seed))
    spreads = {'L0_cond_log_A_real': (-0.6931471824645996, 0.2)}
    factors = {'L0_ffn_b': 4.198, 'L0_ffn_gate_b': 21.954}
    for name, (base, spread) in spreads.items():
        noise = np.random.default_rng([zlib.crc32(name.encode()), seed]).standard_normal(out[name].shape)
        drawn = base * np.exp(spread * noise) if base else spread * noise
        out[name] = jnp.asarray(drawn.astype(out[name].dtype))
    for name, factor in factors.items():
        out[name] = (out[name] * factor).astype(out[name].dtype)
    return out
```

```python
import math
from contextlib import ExitStack

import numpy as np

import concourse.bass as bass
from concourse import mybir
from concourse.alu_op_type import AluOpType as ALU

F32 = mybir.dt.float32
F32R = mybir.dt.float32r
F16 = mybir.dt.float16
I32 = mybir.dt.int32
ACT = mybir.ActivationFunctionType
AX = mybir.AxisListType

P = 128
BATCH, FEATURES, LENGTH = 32, 64, 1024
WAVES = 64
BLOCKS = LENGTH // P
HT = P // BATCH
TILES = FEATURES // HT
HG = 8
GROUPS = FEATURES // HG
QUADS = HG // HT
STEP = 32
RANKS = (8, 16, 32, 64)
RMAX = RANKS[-1]
COLS = LENGTH + RMAX + len(RANKS)
CH = COLS // 3
Z0 = LENGTH - 2 * CH
KROW = P + LENGTH

MAGIC = 12582912.0
LOG2E = 1.0 / math.log(2.0)
LN2_HI = 0.693359375
LN2_LO = math.log(2.0) - LN2_HI
PI2_HI = 6.28125
PI2_MID = float(np.round((2 * math.pi - PI2_HI) * 2**20) / 2**20)
PI2_LO = 2 * math.pi - PI2_HI - PI2_MID
TURN = float(np.nextafter(np.float32(2 * math.pi), np.float32(0)))
EXPONENT_BITS = 0x7F800000


def later(t, n):
    return not isinstance(t, int) or t >= n


def uses(t, u):
    return (t - u) * 8 + 16


def build(nc, x_rows, x_cols, lengths, rates, coefs, skip, weights, bias, lora_b, gate_b, scratch, out):
    with ExitStack() as ctx:
        def sb(name, shape, dt=F32):
            return ctx.enter_context(nc.sbuf_tensor(name, shape, dt))

        def sem(name):
            return ctx.enter_context(nc.semaphore(name))

        swap = sb("swap", [P, P])
        ident = sb("ident", [P, P])
        ramp_i = sb("ramp_i", [P, STEP], I32)
        ramp = sb("ramp", [P, STEP])
        quarter = sb("quarter", [P, 1])
        quarter_rad = sb("quarter_rad", [P, 1])
        quarter_all = sb("quarter_all", [P, 1])
        twice_sign = sb("twice_sign", [P, 1])
        rate = sb("rate", [P, 3, FEATURES])
        coef = sb("coef", [P, 2, FEATURES])
        skip_q = sb("skip_q", [P, TILES])
        len_i = sb("len_i", [P, BATCH], I32)
        len_f = sb("len_f", [P, BATCH])
        pos_i = sb("pos_i", [P, BLOCKS], I32)
        pos_f = sb("pos_f", [P, BLOCKS])
        mask = sb("mask", [P, BLOCKS, BATCH])
        bias_all = sb("bias_all", [P, LENGTH])
        gate_bias = sb("gate_bias", [P, len(RANKS)])
        ex = {n: sb("ex_" + n, [P, 2, FEATURES]) for n in ("k", "r", "p", "e")}
        ex_bits = sb("ex_bits", [P, 2, FEATURES], I32)
        decay = sb("decay", [P, 2, FEATURES])
        theta = sb("theta", [P, 2, FEATURES])
        turns = sb("turns", [P, 2, FEATURES])
        th_k = sb("th_k", [P, 2, FEATURES])
        sm = {n: sb("sm_" + n, [P, FEATURES]) for n in (
            "tanh", "sin", "cos", "den", "em", "zre", "zim", "rabs2", "n1", "n2", "n3", "n4", "nre", "nim", "gre", "gim")}
        phase = sb("phase", [P, 2, 2, HG, STEP])
        whole = sb("whole", [P, 2, HG, STEP])
        wave = sb("wave", [P, GROUPS, 2, HG, STEP])
        mode_re = sb("mode_re", [P, HG, STEP])
        mode_im = sb("mode_im", [P, HG, STEP])
        mode = sb("mode", [P, 2, HG, STEP])
        kern = sb("kern", [P, QUADS, STEP])
        k_top = sb("k_top", [P, 1])
        k_max = sb("k_max", [P, GROUPS])
        k_pow = sb("k_pow", [P, TILES])
        k_rec = sb("k_rec", [P, 1])
        k_scale = sb("k_scale", [P, 1])
        k_parts = sb("k_parts", [P, GROUPS, QUADS, 2, STEP], F16)
        zeros = sb("zeros", [P, P], F16)
        w_raw = sb("w_raw", [P, 2, COLS])
        w_hi = sb("w_hi", [P, BLOCKS, COLS], F32R)
        w_lo = sb("w_lo", [P, BLOCKS, COLS], F32R)
        b_hi = sb("b_hi", [P, LENGTH], F32R)
        b_lo = sb("b_lo", [P, LENGTH], F32R)
        xc = sb("xc", [P, 2, HT, BLOCKS, BATCH])
        x_hi = sb("x_hi", [P, 2, HT, BLOCKS * BATCH], F16)
        x_lo = sb("x_lo", [P, 2, HT, BLOCKS * BATCH], F16)
        x_top = sb("x_top", [P, 2])
        x_max = sb("x_max", [P, 2])
        x_pow = sb("x_pow", [P, 2])
        x_rec = sb("x_rec", [P, 2])
        x_scale = sb("x_scale", [P, 2])
        unscale = sb("unscale", [P, 2])
        toep = sb("toep", [P, 2, 2, HT, LENGTH], F16)
        y = sb("y", [P, BLOCKS, HT, BATCH])
        y_hi = sb("y_hi", [P, 2, BLOCKS, P], F32R)
        y_lo = sb("y_lo", [P, 2, BLOCKS, P], F32R)
        res = sb("res", [P, 2, LENGTH])
        score = sb("score", [P, 4])
        best = sb("best", [P, 1])
        before = sb("before", [P, 8])
        open8 = sb("open8", [P, 8])
        z_open = sb("z_open", [P, 2, RMAX])
        z_parts = sb("z_parts", [P, P], F32R)

        conv = [ctx.enter_context(nc.psum_tensor(f"conv{n}", [P, 2, BLOCKS, BATCH], F32)) for n in range(2)]
        lin = [ctx.enter_context(nc.psum_tensor(f"lin{n}", [P, 512], F32)) for n in range(3)]
        z_turned = ctx.enter_context(nc.psum_tensor("z_turned", [P, 512], F32))
        swapped = ctx.enter_context(nc.psum_tensor("swapped", [P, HG, STEP], F32))
        k_sum = ctx.enter_context(nc.psum_tensor("k_sum", [P, QUADS, HT, STEP], F32))

        params_in, skip_in, len_in, bias_in = map(sem, ("params_in", "skip_in", "len_in", "bias_in"))
        w_in = [sem("w_in0"), sem("w_in1")]
        xc_in = [sem("xc_in0"), sem("xc_in1")]
        xr_in = [sem("xr_in0"), sem("xr_in1")]
        toep_in = [sem("toep_in0"), sem("toep_in1")]
        stored = [sem("stored0"), sem("stored1")]
        pad_out = sem("pad_out")
        k_out = [sem("k_out_first"), sem("k_out_rest")]
        consts_set = sem("consts_set")
        skip_zeroed = sem("skip_zeroed")
        pool_chain = sem("pool_chain")
        dve_chain = sem("dve_chain")
        rates_set = sem("rates_set")
        turns_set = sem("turns_set")
        half_set = sem("half_set")
        damp_arg_set = sem("damp_arg_set")
        damp_set = sem("damp_set")
        wrapped_set = sem("wrapped_set")
        trig_set = sem("trig_set")
        wave_set = sem("wave_set")
        swap_done = sem("swap_done")
        mode_set = sem("mode_set")
        k_summed = sem("k_summed")
        k_top_set = sem("k_top_set")
        k_max_set = sem("k_max_set")
        k_split = sem("k_split")
        w_hi_set, w_lo_set = sem("w_hi_set"), sem("w_lo_set")
        x_top_set, x_max_set, x_scale_set, x_hi_set, x_lo_set = map(
            sem, ("x_top_set", "x_max_set", "x_scale_set", "x_hi_set", "x_lo_set"))
        conv_done = sem("conv_done")
        y_set = sem("y_set")
        y_hi_set, y_lo_set = sem("y_hi_set"), sem("y_lo_set")
        lin_done = [sem(f"lin_done{c}") for c in range(3)]
        z_done = sem("z_done")
        z_open_set = sem("z_open_set")
        z_turn_done = sem("z_turn_done")
        z_hi_set, z_lo_set = sem("z_hi_set"), sem("z_lo_set")
        bias_set = sem("bias_set")
        res_set = sem("res_set")
        share_begun = sem("share_begun")
        x_chain = sem("x_chain")
        unscale_set = sem("unscale_set")
        gate_chain = sem("gate_chain")

        block = ctx.enter_context(nc.Block())

        def bc(ap, axis, shape):
            return ap.unsqueeze(axis).broadcast_to(shape)

        @block.sync
        def _(sp):
            def load_x(t, u):
                if later(t, 2):
                    sp.wait_ge(x_lo_set, t - 1)
                    sp.wait_ge(x_hi_set, t - 1)
                sp.dma_start(xc[:, u], x_cols[t]).then_inc(xc_in[u], 16)

            def load_xr(t, u):
                if later(t, 2):
                    sp.wait_ge(stored[u], uses(t - 2, u))
                sp.dma_start(res[:, u], x_rows[t]).then_inc(xr_in[u], 16)

            def load_toep(t, u):
                if later(t, 2):
                    sp.wait_ge(conv_done, 2 * t - 2)
                src = bass.AP(scratch.tensor, t * (HT * 2 * KROW) + 1, [[1, P], [KROW, 2 * HT], [1, LENGTH]])
                sp.dma_start(toep[:, u].rearrange("p s h n -> p (s h) n"), src).then_inc(toep_in[u], 16)

            def store(t, u):
                sp.wait_ge(res_set, 3 * t + 3)
                sp.dma_start(out[t], res[:, u]).then_inc(stored[u], 16)

            def load_w(k):
                if k >= 2:
                    sp.wait_ge(w_lo_set, k - 1)
                if k < BLOCKS:
                    sp.dma_start(w_raw[:, k % 2], weights[k]).then_inc(w_in[k % 2], 16)
                else:
                    sp.dma_start(w_raw[:, k % 2, 0:LENGTH], lora_b).then_inc(w_in[k % 2], 16)

            sp.dma_start(rate[:], rates).then_inc(params_in, 16)
            sp.dma_start(coef[:], coefs).then_inc(params_in, 16)
            load_x(0, 0)
            sp.dma_start(len_i[:], lengths.partition_broadcast(P)).then_inc(len_in, 16)
            sp.wait_ge(skip_zeroed, 1)
            for j in range(HT):
                sp.dma_start(skip_q[STEP * j:STEP * j + 1, :], skip[j:j + 1, :]).then_inc(skip_in, 16)
            sp.wait_ge(consts_set, 1)
            sp.dma_start(bass.AP(scratch.tensor, 0, [[KROW, 2 * FEATURES], [1, P]]), zeros[:]).then_inc(pad_out, 16)
            load_x(1, 1)
            sp.dma_start(bias_all[:], bias.partition_broadcast(P)).then_inc(bias_in, 16)
            sp.dma_start(gate_bias[:], gate_b.partition_broadcast(P)).then_inc(bias_in, 16)
            load_w(0)
            load_w(1)
            for g in range(GROUPS):
                if g >= 1:
                    load_w(g + 1)
                sp.wait_ge(k_split, g + 1)
                for j in range(HT):
                    dst = bass.AP(scratch.tensor, (g * QUADS * 2 * HT + j) * KROW + P,
                                  [[STEP, STEP], [HT * KROW, 2 * QUADS], [1, STEP]])
                    src = k_parts[STEP * j:STEP * (j + 1), g].rearrange("p q s c -> p (q s) c")
                    sp.dma_start(dst, src).then_inc(k_out[g > 0], 16)
                if g == 0:
                    sp.wait_ge(k_out[0], 16 * HT)
                    sp.wait_ge(pad_out, 16)
                    load_toep(0, 0)
                    load_toep(1, 1)
                    load_xr(0, 0)
                    load_xr(1, 1)
            sp.wait_ge(k_out[1], 16 * HT * (GROUPS - 1))
            with sp.Fori(1, TILES // 2) as i:
                for u in range(2):
                    t = i * 2 + u
                    load_x(t, u)
                    load_toep(t, u)
                    store(t - 2, u)
                    load_xr(t, u)
            for u in range(2):
                store(TILES - 2 + u, u)
            for u in range(2):
                sp.wait_ge(stored[u], 16 * (TILES // 2))

        @block.gpsimd
        def _(pool):
            pool.memset(skip_q[:], 0.0).then_inc(skip_zeroed, 1)
            pool.iota(ramp_i[:], [[1, STEP]], base=0, channel_multiplier=0).then_inc(pool_chain, 1)
            pool.iota(pos_i[:], [[P, BLOCKS]], base=0, channel_multiplier=1).then_inc(pool_chain, 1)
            pool.memset(swap[:], 0.0).then_inc(pool_chain, 1)
            pool.memset(ident[:], 0.0).then_inc(pool_chain, 1)
            pool.wait_ge(pool_chain, 4)
            pool.tensor_copy(ramp[:], ramp_i[:]).then_inc(pool_chain, 1)
            pool.tensor_copy(pos_f[:], pos_i[:]).then_inc(pool_chain, 1)
            pool.affine_select(out=swap[:], in_=swap[:], compare_op=ALU.not_equal, fill=1.0, base=WAVES,
                               pattern=[[-1, P]], channel_multiplier=1).then_inc(pool_chain, 1)
            pool.affine_select(out=ident[:], in_=ident[:], compare_op=ALU.not_equal, fill=1.0, base=0,
                               pattern=[[-1, P]], channel_multiplier=1).then_inc(pool_chain, 1)
            pool.wait_ge(pool_chain, 8)
            pool.affine_select(out=swap[:], in_=swap[:], compare_op=ALU.not_equal, fill=-1.0, base=-WAVES,
                               pattern=[[-1, P]], channel_multiplier=1).then_inc(pool_chain, 1)
            pool.memset(zeros[:], 0.0).then_inc(pool_chain, 1)
            pool.memset(before[:, 0:1], -3.0e38).then_inc(pool_chain, 1)
            pool.wait_ge(pool_chain, 11)
            pool.engine_nop().then_inc(consts_set, 1)

            for g in range(GROUPS):
                if g == 0:
                    pool.wait_ge(rates_set, 1)
                for s in range(2):
                    ins = pool.tensor_tensor(
                        wave[:, g, s], bc(decay[:, s, g * HG:(g + 1) * HG], 2, [P, HG, STEP]),
                        bc(ramp[:], 1, [P, HG, STEP]), ALU.mult)
                ins.then_inc(damp_arg_set, 1)

            def share_k(g):
                pool.wait_ge(k_top_set, g + 1)
                pool.partition_all_reduce(k_max[:, g:g + 1], k_top[:], P, bass.bass_isa.ReduceOp.max)\
                    .then_inc(k_max_set, 1)

            def share_x(t, u):
                pool.wait_ge(x_top_set, t + 1)
                if later(t, 2):
                    pool.wait_ge(x_scale_set, t - 1)
                pool.sem_inc(share_begun, 1)
                pool.partition_all_reduce(x_max[:, u:u + 1], x_top[:, u:u + 1], P, bass.bass_isa.ReduceOp.max)\
                    .then_inc(x_max_set, 1)

            def split_y(t, u):
                pool.wait_ge(y_hi_set, t + 1)
                if later(t, 2):
                    pool.wait_ge(lin_done[1], t - 1)
                pool.tensor_tensor(y_lo[:, u], y[:].rearrange("p i h b -> p i (h b)"), y_hi[:, u].bitcast(F32),
                                   ALU.subtract).then_inc(y_lo_set, 1)

            def add_bias(t, u):
                pool.wait_ge(xr_in[u], uses(t, u))
                pool.tensor_tensor(res[:, u], res[:, u], bias_all[:], ALU.add).then_inc(bias_set, 1)

            share_x(0, 0)
            for k in range(BLOCKS):
                share_k(k)
                if k == 0:
                    share_x(1, 1)
                pool.wait_ge(w_hi_set, k + 1)
                pool.tensor_tensor(w_lo[:, k], w_raw[:, k % 2], w_hi[:, k].bitcast(F32), ALU.subtract)\
                    .then_inc(w_lo_set, 1)
            pool.wait_ge(w_hi_set, BLOCKS + 1)
            pool.tensor_tensor(b_lo[:], w_raw[:, BLOCKS % 2, 0:LENGTH], b_hi[:].bitcast(F32), ALU.subtract)\
                .then_inc(w_lo_set, 1)
            pool.wait_ge(bias_in, 32)

            def step(t, u):
                if not isinstance(t, int) or 2 <= t + 1 < TILES:
                    share_x(t + 1, 1 - u)
                split_y(t, u)
                add_bias(t, u)

            for t in range(2):
                step(t, t)
            with pool.Fori(1, TILES // 2 - 1) as i:
                for u in range(2):
                    step(i * 2 + u, u)
            for u in range(2):
                step(TILES - 2 + u, u)

        @block.scalar
        def _(act):
            act.wait_ge(rates_set, 1)
            act.activation(sm["tanh"][:], decay[:, 0], ACT.Tanh, scale=0.5).then_inc(half_set, 1)
            for g in range(GROUPS):
                act.wait_ge(damp_arg_set, g + 1)
                act.activation(wave[:, g], wave[:, g], ACT.Exp).then_inc(damp_set, 1)
            act.wait_ge(turns_set, 1)
            act.wait_ge(consts_set, 1)
            act.activation(sm["sin"][:], turns[:, 0], ACT.Sin, scale=0.5 * TURN).then_inc(half_set, 1)
            act.activation(sm["cos"][:], turns[:, 0], ACT.Sin, bias=quarter_all[:], scale=0.5 * TURN)\
                .then_inc(half_set, 1)

            def split_x(t, u):
                act.wait_ge(x_scale_set, t + 1)
                if later(t, 2):
                    act.wait_ge(conv_done, 2 * t - 2)
                act.activation(x_hi[:, u], xc[:, u].rearrange("p h i b -> p h (i b)"), ACT.Copy,
                               scale=x_scale[:, u:u + 1]).then_inc(x_hi_set, 1)

            def split_y(t, u):
                act.wait_ge(y_set, 2 * t + 2)
                if later(t, 2):
                    act.wait_ge(lin_done[1], t - 1)
                act.activation(y_hi[:, u], y[:].rearrange("p i h b -> p i (h b)"), ACT.Copy).then_inc(y_hi_set, 1)

            def split_z(t):
                act.wait_ge(z_turn_done, t + 1)
                if later(t, 1):
                    act.wait_ge(lin_done[1], t)
                act.activation(z_parts[:], z_turned[:, 0:P], ACT.Copy).then_inc(z_hi_set, 1)

            for g in range(GROUPS):
                act.wait_ge(wrapped_set, g + 1)
                act.activation(phase[:, g % 2], phase[:, g % 2], ACT.Sin, bias=quarter_rad[:], scale=-TURN)\
                    .then_inc(trig_set, 1)
                if g == 1:
                    split_x(0, 0)
                if g == 3:
                    split_x(1, 1)
                act.wait_ge(w_in[g % 2], 16 * (g // 2 + 1))
                act.activation(w_hi[:, g], w_raw[:, g % 2], ACT.Copy).then_inc(w_hi_set, 1)
            act.wait_ge(w_in[BLOCKS % 2], 16 * (BLOCKS // 2 + 1))
            act.activation(b_hi[:], w_raw[:, BLOCKS % 2, 0:LENGTH], ACT.Copy).then_inc(w_hi_set, 1)

            def step(t, u):
                if not isinstance(t, int) or 2 <= t + 1 < TILES:
                    split_x(t + 1, 1 - u)
                if not isinstance(t, int) or t < TILES:
                    split_y(t, u)
                if later(t, 1):
                    split_z(t - 1)

            for t in range(2):
                step(t, t)
            with act.Fori(1, TILES // 2 - 1) as i:
                for u in range(2):
                    step(i * 2 + u, u)
            for t in range(TILES - 2, TILES + 1):
                step(t, t % 2)

        @block.tensor
        def _(pe):
            def swap_waves(g):
                pe.wait_ge(wave_set, g + 1)
                if g == 0:
                    pe.wait_ge(consts_set, 1)
                if g >= 1:
                    pe.wait_ge(mode_set, g)
                pe.matmul(swapped[:], swap[:], wave[:, g, 1], start=True, stop=True).then_inc(swap_done, 1)

            def sum_waves(g):
                pe.wait_ge(mode_set, g + 1)
                if g >= 1:
                    pe.wait_ge(k_top_set, g)
                for q in range(QUADS):
                    mm = pe.matmul(k_sum[:, q], mode[:, g % 2, HT * q:HT * q + HT], wave[:, g, 0, HT * q:HT * q + HT],
                                   start=True, stop=True)
                mm.then_inc(k_summed, 1)

            def convolve(t, u):
                pe.wait_ge(x_lo_set, t + 1)
                pe.wait_ge(toep_in[u], uses(t, u))
                for h in range(HT):
                    if h % 2 == 0 and later(t, 1):
                        pe.wait_ge(y_set, 2 * t - 1 + h // 2)
                    for d in range(BLOCKS):
                        n = (BLOCKS - d) * BATCH
                        for part, x in ((0, x_hi), (0, x_lo), (1, x_hi)):
                            mm = pe.matmul(conv[h // 2][:, h % 2, d:BLOCKS], toep[:, u, part, h, d * P:(d + 1) * P],
                                           x[:, u, h, 0:n], start=(d == 0 and part == 0 and x is x_hi),
                                           stop=(d == BLOCKS - 1 and part == 1))
                    if h % 2 == 1:
                        mm.then_inc(conv_done, 1)

            def linear(t, u):
                pe.wait_ge(y_lo_set, t + 1)
                if isinstance(t, int) and t == 0:
                    pe.wait_ge(w_lo_set, BLOCKS + 1)
                for n, c in enumerate((2, 0, 1)):
                    if later(t, 1):
                        pe.wait_ge(res_set, 3 * t - 2 + n)
                    for k in range(BLOCKS):
                        for first, second in ((y_hi, w_hi), (y_hi, w_lo), (y_lo, w_hi)):
                            mm = pe.matmul(lin[c][:, 0:CH], first[:, u, k], second[:, k, c * CH:(c + 1) * CH],
                                           start=(k == 0 and first is y_hi and second is w_hi),
                                           stop=(k == BLOCKS - 1 and first is y_lo))
                    if c == 2:
                        mm.then_inc(z_done, 1)
                    if c == 0:
                        pe.wait_ge(z_open_set, t + 1)
                        if later(t, 1):
                            pe.wait_ge(z_lo_set, t)
                        pe.transpose(z_turned[:, 0:P], z_open[:], ident[:]).then_inc(z_turn_done, 1)
                pe.wait_ge(z_lo_set, t + 1)
                for c in (2, 0, 1):
                    w = Z0 if c == 2 else CH
                    for rows, b in ((P, b_hi), (RMAX, b_lo)):
                        mm = pe.matmul(lin[c][:, 0:w], z_parts[0:rows], b[0:rows, c * CH:c * CH + w],
                                       start=False, stop=True, skip_group_check=True)
                    mm.then_inc(lin_done[c], 1)

            for g in range(GROUPS):
                swap_waves(g)
                sum_waves(g)
            convolve(0, 0)
            convolve(1, 1)
            linear(0, 0)
            with pe.Fori(1, TILES // 2) as i:
                for u in range(2):
                    convolve(i * 2 + u, u)
                    linear(i * 2 + u - 1, 1 - u)
            linear(TILES - 1, 1)

        @block.vector
        def _(dve):
            chained = [0]

            def link(ins):
                ins.then_inc(dve_chain, 1)
                chained[0] += 1

            def settle():
                dve.wait_ge(dve_chain, chained[0])

            for tile, upper, lower in ((quarter, 0.25, 0.0), (quarter_rad, 0.25 * TURN, 0.0), (twice_sign, 2.0, -2.0)):
                link(dve.memset(tile[0:WAVES], upper))
                link(dve.memset(tile[WAVES:P], lower))
            link(dve.memset(quarter_all[:], 0.25 * TURN))
            dve.wait_ge(params_in, 32)
            arg = rate[:, 0:2]
            link(dve.tensor_scalar(ex["k"][:], arg, LOG2E, MAGIC, ALU.mult, ALU.add))
            settle()
            link(dve.tensor_scalar(ex["k"][:], ex["k"][:], MAGIC, None, ALU.subtract))
            settle()
            link(dve.scalar_tensor_tensor(out=ex["r"][:], in0=ex["k"][:], scalar=-LN2_HI, in1=arg, op0=ALU.mult, op1=ALU.add))
            settle()
            link(dve.scalar_tensor_tensor(out=ex["r"][:], in0=ex["k"][:], scalar=-LN2_LO, in1=ex["r"][:],
                                          op0=ALU.mult, op1=ALU.add))
            link(dve.tensor_scalar(ex["k"][:], ex["k"][:], 126.0, -126.0, ALU.min, ALU.max))
            settle()
            link(dve.tensor_scalar(ex_bits[:], ex["k"][:], 127.0, float(1 << 23), ALU.add, ALU.mult))
            link(dve.tensor_scalar(ex["p"][:], ex["r"][:], 1.0 / math.factorial(7), None, ALU.mult))
            for n in range(6, 0, -1):
                settle()
                link(dve.scalar_tensor_tensor(out=ex["p"][:], in0=ex["p"][:], scalar=1.0 / math.factorial(n),
                                              in1=ex["r"][:], op0=ALU.add, op1=ALU.mult))
            settle()
            link(dve.scalar_tensor_tensor(out=ex["e"][:], in0=ex["p"][:], scalar=1.0, in1=ex_bits[:].bitcast(F32),
                                          op0=ALU.add, op1=ALU.mult))
            settle()
            dt, ar, ai = ex["e"][:, 0], ex["e"][:, 1], rate[:, 2]
            link(dve.scalar_tensor_tensor(out=decay[:, 0], in0=ar, scalar=-1.0, in1=dt, op0=ALU.mult, op1=ALU.mult))
            link(dve.tensor_tensor(theta[:, 0], ai, dt, ALU.mult))
            settle()
            link(dve.tensor_scalar(theta[:, 1], theta[:, 0], float(STEP), None, ALU.mult))
            dve.tensor_scalar(decay[:, 1], decay[:, 0], float(STEP), None, ALU.mult).then_inc(rates_set, 1)
            settle()
            link(dve.tensor_scalar(th_k[:], theta[:], 1.0 / (2 * math.pi), MAGIC, ALU.mult, ALU.add))
            settle()
            link(dve.tensor_scalar(th_k[:], th_k[:], MAGIC, None, ALU.subtract))
            for part in (PI2_HI, PI2_MID, PI2_LO):
                settle()
                link(dve.scalar_tensor_tensor(out=theta[:], in0=th_k[:], scalar=-part, in1=theta[:],
                                              op0=ALU.mult, op1=ALU.add))
            settle()
            dve.tensor_scalar(turns[:], theta[:], 1.0 / (2 * math.pi), None, ALU.mult).then_inc(turns_set, 1)
            dve.wait_ge(turns_set, 1)
            dve.wait_ge(consts_set, 1)

            def wrap_phases(g):
                ph = phase[:, g % 2]
                for s in range(2):
                    link(dve.tensor_tensor(ph[:, s], bc(turns[:, s, g * HG:(g + 1) * HG], 2, [P, HG, STEP]),
                                           bc(ramp[:], 1, [P, HG, STEP]), ALU.mult))
                settle()
                link(dve.tensor_scalar(whole[:], ph, quarter[:], MAGIC, ALU.add, ALU.add))
                settle()
                dve.scalar_tensor_tensor(out=ph, in0=whole[:], scalar=MAGIC, in1=ph,
                                         op0=ALU.subtract, op1=ALU.subtract).then_inc(wrapped_set, 1)

            def top_x(t, u):
                dve.wait_ge(xc_in[u], uses(t, u))
                dve.tensor_reduce(x_top[:, u:u + 1], xc[:, u].rearrange("p h i b -> p (h i b)"), AX.X, ALU.max,
                                  apply_absolute_value=True).then_inc(x_top_set, 1)

            def scale_x(t, u):
                dve.wait_ge(x_max_set, t + 1)
                dve.tensor_scalar(x_pow[:, u:u + 1], x_max[:, u:u + 1], 2.0**-60, None, ALU.max).then_inc(x_chain, 1)
                dve.wait_ge(x_chain, 3 * t + 1)
                dve.tensor_scalar(x_pow[:, u:u + 1].bitcast(I32), x_pow[:, u:u + 1].bitcast(I32), EXPONENT_BITS, None,
                                  ALU.bitwise_and).then_inc(x_chain, 1)
                dve.wait_ge(x_chain, 3 * t + 2)
                dve.reciprocal(x_rec[:, u:u + 1], x_pow[:, u:u + 1]).then_inc(x_chain, 1)
                dve.wait_ge(x_chain, 3 * t + 3)
                dve.tensor_scalar(x_scale[:, u:u + 1], x_rec[:, u:u + 1], 2.0**14, None, ALU.mult)\
                    .then_inc(x_scale_set, 1)

            def split_x(t, u):
                dve.wait_ge(x_hi_set, t + 1)
                dve.scalar_tensor_tensor(
                    out=x_lo[:, u].rearrange("p h n -> p (h n)"), in0=xc[:, u].rearrange("p h i b -> p (h i b)"),
                    scalar=x_scale[:, u:u + 1], in1=x_hi[:, u].rearrange("p h n -> p (h n)"), op0=ALU.mult,
                    op1=ALU.subtract).then_inc(x_lo_set, 1)

            wrap_phases(0)
            wrap_phases(1)
            top_x(0, 0)
            dve.wait_ge(half_set, 3)
            s = {n: v[:] for n, v in sm.items()}
            tt = dve.tensor_tensor

            def stt(o, a, scalar, b, op0, op1):
                return dve.scalar_tensor_tensor(out=o, in0=a, scalar=scalar, in1=b, op0=op0, op1=op1)

            link(dve.tensor_scalar(s["den"], s["tanh"], -1.0, 1.0, ALU.mult, ALU.add))
            link(tt(s["n1"], s["sin"], s["sin"], ALU.mult))
            link(tt(s["n2"], s["sin"], s["cos"], ALU.mult))
            link(tt(s["n3"], ar, ar, ALU.mult))
            link(tt(s["n4"], ai, ai, ALU.mult))
            settle()
            link(dve.reciprocal(s["den"], s["den"]))
            link(tt(s["rabs2"], s["n3"], s["n4"], ALU.add))
            settle()
            link(stt(s["em"], s["tanh"], 2.0, s["den"], ALU.mult, ALU.mult))
            link(dve.reciprocal(s["rabs2"], s["rabs2"]))
            settle()
            link(stt(s["n3"], s["em"], 1.0, s["n1"], ALU.add, ALU.mult))
            link(stt(s["n4"], s["em"], 1.0, s["n2"], ALU.add, ALU.mult))
            settle()
            link(stt(s["zre"], s["n3"], -2.0, s["em"], ALU.mult, ALU.add))
            link(dve.tensor_scalar(s["zim"], s["n4"], 2.0, None, ALU.mult))
            settle()
            link(tt(s["n1"], ar, s["zre"], ALU.mult))
            link(tt(s["n2"], ai, s["zim"], ALU.mult))
            link(stt(s["n3"], s["zim"], -1.0, ar, ALU.mult, ALU.mult))
            link(tt(s["n4"], ai, s["zre"], ALU.mult))
            settle()
            link(tt(s["nre"], s["n2"], s["n1"], ALU.subtract))
            link(tt(s["nim"], s["n3"], s["n4"], ALU.subtract))
            settle()
            cre, cim = coef[:, 0], coef[:, 1]
            link(tt(s["n1"], cre, s["nre"], ALU.mult))
            link(tt(s["n2"], cim, s["nim"], ALU.mult))
            link(tt(s["n3"], cre, s["nim"], ALU.mult))
            link(tt(s["n4"], cim, s["nre"], ALU.mult))
            settle()
            link(tt(s["zre"], s["n1"], s["n2"], ALU.subtract))
            link(tt(s["zim"], s["n3"], s["n4"], ALU.add))
            settle()
            link(stt(s["gre"], s["zre"], twice_sign[:], s["rabs2"], ALU.mult, ALU.mult))
            link(stt(s["gim"], s["zim"], twice_sign[:], s["rabs2"], ALU.mult, ALU.mult))
            scale_x(0, 0)
            settle()

            def finish_waves(g):
                dve.wait_ge(trig_set, g + 1)
                dve.wait_ge(damp_set, g + 1)
                dve.tensor_tensor(wave[:, g], wave[:, g], phase[:, g % 2], ALU.mult).then_inc(wave_set, 1)

            def weigh_waves(g):
                dve.wait_ge(wave_set, g + 1)
                cols = slice(g * HG, (g + 1) * HG)
                link(tt(mode_re[:], wave[:, g, 1], bc(sm["gre"][:, cols], 2, [P, HG, STEP]), ALU.mult))
                dve.wait_ge(swap_done, g + 1)
                link(tt(mode_im[:], swapped[:], bc(sm["gim"][:, cols], 2, [P, HG, STEP]), ALU.mult))
                settle()
                tt(mode[:, g % 2], mode_re[:], mode_im[:], ALU.add).then_inc(mode_set, 1)

            def take_kernels(g):
                dve.wait_ge(k_summed, g + 1)
                for j in range(HT):
                    link(dve.tensor_copy(kern[STEP * j:STEP * (j + 1)], k_sum[STEP * j:STEP * (j + 1), :, j]))
                settle()
                link(tt(kern[:, :, 0], kern[:, :, 0], skip_q[:, g * QUADS:(g + 1) * QUADS], ALU.add))
                settle()
                dve.tensor_reduce(k_top[:], kern[:].rearrange("p q c -> p (q c)"), AX.X, ALU.max,
                                  apply_absolute_value=True).then_inc(k_top_set, 1)

            def split_kernels(g):
                dve.wait_ge(k_max_set, g + 1)
                kp = k_pow[:, g * QUADS:(g + 1) * QUADS]
                link(dve.tensor_scalar(kp, k_max[:, g:g + 1].broadcast_to([P, QUADS]), 2.0**-60, None, ALU.max))
                settle()
                link(dve.tensor_scalar(kp.bitcast(I32), kp.bitcast(I32), EXPONENT_BITS, None, ALU.bitwise_and))
                settle()
                link(dve.reciprocal(k_rec[:], kp[:, 0:1]))
                settle()
                link(dve.tensor_scalar(k_scale[:], k_rec[:], 2.0**14, None, ALU.mult))
                settle()
                link(dve.tensor_scalar(k_parts[:, g, :, 0], kern[:], k_scale[:], None, ALU.mult))
                settle()
                stt(k_parts[:, g, :, 1], kern[:], k_scale[:], k_parts[:, g, :, 0], ALU.mult, ALU.subtract).then_inc(k_split, 1)

            dve.wait_ge(skip_in, 16 * HT)
            for g in range(GROUPS):
                finish_waves(g)
                if g + 2 < GROUPS:
                    dve.wait_ge(wave_set, g + 1)
                    wrap_phases(g + 2)
                weigh_waves(g)
                take_kernels(g)
                if g == 0:
                    split_x(0, 0)
                    top_x(1, 1)
                if g == 1:
                    scale_x(1, 1)
                if g == 3:
                    split_x(1, 1)
                split_kernels(g)

            dve.wait_ge(len_in, 16)
            link(dve.tensor_copy(len_f[:], len_i[:]))
            settle()
            link(tt(mask[:], bc(pos_f[:], 2, [P, BLOCKS, BATCH]), bc(len_f[:], 1, [P, BLOCKS, BATCH]), ALU.is_lt))
            settle()
            dve.wait_ge(bias_in, 32)

            def take_y(t, u, n):
                if n == 0:
                    stt(unscale[:, u:u + 1], x_pow[:, u:u + 1], 2.0**-28, k_pow[:, bass.ds(t, 1)], ALU.mult, ALU.mult)\
                        .then_inc(unscale_set, 1)
                    dve.wait_ge(unscale_set, t + 1)
                    if later(t, 1):
                        dve.wait_ge(y_lo_set, t)
                dve.wait_ge(conv_done, 2 * t + n + 1)
                for h in range(2):
                    ins = stt(y[:, :, 2 * n + h], conv[n][:, h], unscale[:, u:u + 1], mask[:], ALU.mult, ALU.mult)
                ins.then_inc(y_set, 1)

            def pick_rank(t):
                z = lin[2][:, Z0:Z0 + RMAX]
                dve.wait_ge(z_done, t + 1)
                tt(score[:], lin[2][:, Z0 + RMAX:Z0 + RMAX + 4], gate_bias[:], ALU.add).then_inc(gate_chain, 1)
                dve.wait_ge(gate_chain, 4 * t + 1)
                dve.tensor_reduce(best[:], score[:], AX.X, ALU.max)
                dve.tensor_copy(before[:, 1:2], score[:, 0:1])
                tt(before[:, 2:4], score[:, 0:1].broadcast_to([P, 2]), score[:, 1:2].broadcast_to([P, 2]), ALU.max)\
                    .then_inc(gate_chain, 1)
                dve.wait_ge(gate_chain, 4 * t + 2)
                tt(before[:, 4:8], before[:, 2:3].broadcast_to([P, 4]), score[:, 2:3].broadcast_to([P, 4]), ALU.max)\
                    .then_inc(gate_chain, 1)
                dve.wait_ge(gate_chain, 4 * t + 3)
                dve.tensor_scalar(open8[:], before[:], best[:], None, ALU.is_lt).then_inc(gate_chain, 1)
                dve.wait_ge(gate_chain, 4 * t + 4)
                if later(t, 1):
                    dve.wait_ge(z_turn_done, t)
                for twice in range(2):
                    ins = tt(z_open[:, twice].rearrange("p (g c) -> p g c", g=8), z.rearrange("p (g c) -> p g c", g=8),
                             bc(open8[:], 2, [P, 8, 8]), ALU.mult)
                ins.then_inc(z_open_set, 1)

            def split_z(t):
                dve.wait_ge(z_hi_set, t + 1)
                tt(z_parts[RMAX:P], z_turned[RMAX:P, 0:P], z_parts[RMAX:P].bitcast(F32), ALU.subtract)\
                    .then_inc(z_lo_set, 1)

            def finish(t, u):
                dve.wait_ge(bias_set, t + 1)
                for c in (2, 0, 1):
                    w = Z0 if c == 2 else CH
                    dve.wait_ge(lin_done[c], t + 1)
                    tt(res[:, u, c * CH:c * CH + w], res[:, u, c * CH:c * CH + w], lin[c][:, 0:w], ALU.add)\
                        .then_inc(res_set, 1)

            def step(t, u):
                more = not isinstance(t, int) or 2 <= t + 1 < TILES
                tile = not isinstance(t, int) or t < TILES
                if more:
                    top_x(t + 1, 1 - u)
                if tile:
                    take_y(t, u, 0)
                if more:
                    scale_x(t + 1, 1 - u)
                if tile:
                    take_y(t, u, 1)
                if more:
                    split_x(t + 1, 1 - u)
                if later(t, 1):
                    pick_rank(t - 1)
                    split_z(t - 1)
                    finish(t - 1, 1 - u)

            for t in range(2):
                step(t, t)
            with dve.Fori(1, TILES // 2 - 1) as i:
                for u in range(2):
                    step(i * 2 + u, u)
            for t in range(TILES - 2, TILES + 1):
                step(t, t % 2)


def kernel(x, itok_B_8_3872, L0_cond_log_dt, L0_cond_C, L0_cond_log_A_real, L0_cond_A_imag, L0_cond_D,
           L0_ffn_W, L0_ffn_b, L0_ffn_A, L0_ffn_B, L0_ffn_gate_w, L0_ffn_gate_b):
    import concourse.bacc as bacc
    from concourse.bass_utils import run_bass_kernel_spmd

    def lay(a):
        return np.ascontiguousarray(a)

    x = np.asarray(x)
    x_rows = lay(x.transpose(1, 0, 2).reshape(TILES, P, LENGTH))
    x_cols = lay(x.reshape(BATCH, TILES, HT, BLOCKS, P)[..., ::-1].transpose(1, 4, 2, 3, 0))
    twice = lambda a: np.concatenate([a, a])
    log_dt = np.broadcast_to(np.asarray(L0_cond_log_dt), (WAVES, FEATURES))
    rates = lay(twice(np.stack([log_dt, np.asarray(L0_cond_log_A_real).T, np.asarray(L0_cond_A_imag).T], 1)))
    coefs = lay(twice(np.asarray(L0_cond_C).transpose(1, 2, 0)))
    skip = lay(np.asarray(L0_cond_D).reshape(TILES, HT).T)
    weights = lay(np.concatenate([np.asarray(a) for a in (L0_ffn_W, L0_ffn_A, L0_ffn_gate_w)]).T
                  .reshape(BLOCKS, P, COLS))
    lora_b = lay(twice(np.asarray(L0_ffn_B).T))

    nc = bacc.Bacc("TRN2", target_bir_lowering=False, num_devices=1)
    arrays = {
        "x_rows": x_rows, "x_cols": x_cols, "lengths": lay(itok_B_8_3872), "rates": rates, "coefs": coefs,
        "skip": skip, "weights": weights, "bias": lay(L0_ffn_b), "lora_b": lora_b, "gate_b": lay(L0_ffn_gate_b),
    }
    args = [nc.dram_tensor(n, a.shape, mybir.dt.from_np(a.dtype), kind="ExternalInput").ap() for n, a in arrays.items()]
    scratch = nc.dram_tensor("kernels", (TILES, 2, HT, KROW), F16, kind="Internal").ap()
    out = nc.dram_tensor("out", (TILES, P, LENGTH), F32, kind="ExternalOutput").ap()
    build(nc, *args, scratch, out)
    r = run_bass_kernel_spmd(nc, [arrays], core_ids=[0])
    return r.results[0]["out"].reshape(FEATURES, BATCH, LENGTH).transpose(1, 0, 2)
```

```python
import math
from contextlib import ExitStack

import numpy as np

import concourse.bass as bass
from concourse import mybir
from concourse.alu_op_type import AluOpType as ALU

F32 = mybir.dt.float32
F32R = mybir.dt.float32r
F16 = mybir.dt.float16
BF16 = mybir.dt.bfloat16
I32 = mybir.dt.int32
ACT = mybir.ActivationFunctionType
AX = mybir.AxisListType

P = 128
BATCH, FEATURES, LENGTH = 32, 64, 1024
WAVES = 64
BLOCKS = LENGTH // P
HT = P // BATCH
TILES = FEATURES // HT
HG = 8
GROUPS = FEATURES // HG
QUADS = HG // HT
STEP = 32
RANKS = (8, 16, 32, 64)
RMAX = RANKS[-1]
COLS = LENGTH + RMAX + len(RANKS)
CH = COLS // 3
Z0 = LENGTH - 2 * CH
KROW = P + LENGTH
RAW = 4
W_BEFORE_GROUP_1 = 6

MAGIC = 12582912.0
LOG2E = 1.0 / math.log(2.0)
LN2_HI = 0.693359375
LN2_LO = math.log(2.0) - LN2_HI
PI2_HI = 6.28125
PI2_MID = float(np.round((2 * math.pi - PI2_HI) * 2**20) / 2**20)
PI2_LO = 2 * math.pi - PI2_HI - PI2_MID
TURN = float(np.nextafter(np.float32(2 * math.pi), np.float32(0)))
EXPONENT_BITS = 0x7F800000


def later(t, n):
    return not isinstance(t, int) or t >= n


def known(n, below):
    return not isinstance(n, int) or 0 <= n < below


def uses(t, u):
    return (t - u) * 8 + 16


def build(nc, x_rows, x_cols, lengths, rates, coefs, skip, weights, bias, lora_b, gate_b, scratch, out):
    with ExitStack() as ctx:
        def sb(name, shape, dt=F32):
            return ctx.enter_context(nc.sbuf_tensor(name, shape, dt))

        def sem(name):
            return ctx.enter_context(nc.semaphore(name))

        swap = sb("swap", [P, P])
        ident = sb("ident", [P, P])
        ramp_i = sb("ramp_i", [P, STEP], I32)
        ramp = sb("ramp", [P, STEP])
        quarter = sb("quarter", [P, 1])
        quarter_rad = sb("quarter_rad", [P, 1])
        quarter_all = sb("quarter_all", [P, 1])
        twice_sign = sb("twice_sign", [P, 1])
        rate = sb("rate", [P, 4, FEATURES])
        coef = sb("coef", [P, 2, FEATURES])
        skip_q = sb("skip_q", [P, TILES])
        ones = sb("ones", [P, P], BF16)
        len_i = sb("len_i", [P, BATCH], I32)
        len_f = sb("len_f", [P, BATCH])
        pos_i = sb("pos_i", [P, BLOCKS], I32)
        pos_f = sb("pos_f", [P, BLOCKS])
        mask = sb("mask", [P, BLOCKS, BATCH])
        bias_all = sb("bias_all", [P, LENGTH])
        gate_bias = sb("gate_bias", [P, len(RANKS)])
        ex = {n: sb("ex_" + n, [P, 2, FEATURES]) for n in ("k", "r", "p", "e")}
        ex_bits = sb("ex_bits", [P, 2, FEATURES], I32)
        decay = sb("decay", [P, 2, FEATURES])
        theta = sb("theta", [P, 2, FEATURES])
        turns = sb("turns", [P, 2, FEATURES])
        th_k = sb("th_k", [P, 2, FEATURES])
        sm = {n: sb("sm_" + n, [P, FEATURES]) for n in (
            "tanh", "sin", "cos", "den", "em", "zre", "zim", "rabs2", "n1", "n2", "n3", "n4", "nre", "nim", "gre", "gim")}
        phase = sb("phase", [P, 2, HG, STEP])
        whole = sb("whole", [P, 2, HG, STEP])
        wave = sb("wave", [P, 2, HG, STEP])
        mode_re = sb("mode_re", [P, HG, STEP])
        mode_im = sb("mode_im", [P, HG, STEP])
        mode = sb("mode", [P, HG, STEP])
        kern = sb("kern", [P, QUADS, STEP])
        k_sizes = sb("k_sizes", [P, FEATURES], BF16)
        k_bound = sb("k_bound", [P, FEATURES])
        k_pow = sb("k_pow", [P, TILES])
        k_scale = sb("k_scale", [P, TILES])
        k_parts = sb("k_parts", [P, QUADS, 2, STEP], F16)
        zeros = sb("zeros", [P, P], F16)
        w_raw = sb("w_raw", [P, RAW, COLS])
        w_hi = sb("w_hi", [P, BLOCKS, COLS], F32R)
        w_lo = sb("w_lo", [P, BLOCKS, COLS], F32R)
        b_hi = sb("b_hi", [P, LENGTH], F32R)
        b_lo = sb("b_lo", [P, LENGTH], F32R)
        xc = sb("xc", [P, 2, HT, BLOCKS, BATCH])
        x_hi = sb("x_hi", [P, 2, HT, BLOCKS * BATCH], F16)
        x_lo = sb("x_lo", [P, 2, HT, BLOCKS * BATCH], F16)
        x_top = sb("x_top", [P, 2], BF16)
        x_pow = sb("x_pow", [P, 2])
        x_rec = sb("x_rec", [P, 2])
        x_scale = sb("x_scale", [P, 2])
        unscale = sb("unscale", [P, 2])
        toep = sb("toep", [P, 2, 2, HT, LENGTH], F16)
        y = sb("y", [P, BLOCKS, HT, BATCH])
        y_hi = sb("y_hi", [P, 2, BLOCKS, P], F32R)
        y_lo = sb("y_lo", [P, 2, BLOCKS, P], F32R)
        res = sb("res", [P, 2, LENGTH])
        score = sb("score", [P, 4])
        best = sb("best", [P, 1])
        before = sb("before", [P, 8])
        open8 = sb("open8", [P, 8])
        z_open = sb("z_open", [P, 2, RMAX])
        z_parts = sb("z_parts", [P, P], F32R)

        conv = [ctx.enter_context(nc.psum_tensor(f"conv{n}", [P, 2, BLOCKS, BATCH], F32)) for n in range(2)]
        lin = [ctx.enter_context(nc.psum_tensor(f"lin{n}", [P, 512], F32)) for n in range(3)]
        z_turned = ctx.enter_context(nc.psum_tensor("z_turned", [P, 512], F32))
        swapped = ctx.enter_context(nc.psum_tensor("swapped", [P, HG * STEP + 2], F32))
        k_sum = ctx.enter_context(nc.psum_tensor("k_sum", [P, QUADS, HT, STEP], F32))
        x_sum = swapped[:, HG * STEP:]

        params_in, skip_in, len_in, bias_in = map(sem, ("params_in", "skip_in", "len_in", "bias_in"))
        w_in = [sem(f"w_in{k}") for k in range(0, BLOCKS + 1, 2)]
        xc_in = [sem("xc_in0"), sem("xc_in1")]
        xr_in = [sem("xr_in0"), sem("xr_in1")]
        toep_in = [sem("toep_in0"), sem("toep_in1")]
        stored = [sem("stored0"), sem("stored1")]
        pad_out = sem("pad_out")
        toep_first = [sem(f"toep_first{h}") for h in range(HT)]
        k_out = sem("k_out")
        consts_set = sem("consts_set")
        skip_zeroed = sem("skip_zeroed")
        pool_chain = sem("pool_chain")
        dve_chain = sem("dve_chain")
        rates_set = sem("rates_set")
        turns_set = sem("turns_set")
        half_set = sem("half_set")
        damp_arg_set = sem("damp_arg_set")
        phase_set = sem("phase_set")
        damp_set = sem("damp_set")
        whole_set = sem("whole_set")
        wrapped_set = sem("wrapped_set")
        trig_set = sem("trig_set")
        wave_set = sem("wave_set")
        swap_done = sem("swap_done")
        mode_chain = sem("mode_chain")
        mode_set = sem("mode_set")
        k_summed = sem("k_summed")
        kern_chain = sem("kern_chain")
        k_split = sem("k_split")
        sizes_set, bound_done = sem("sizes_set"), sem("bound_done")
        w_hi_set, w_lo_set = sem("w_hi_set"), sem("w_lo_set")
        x_top_set, x_sum_done, x_scale_set, x_hi_set, x_lo_set = map(
            sem, ("x_top_set", "x_sum_done", "x_scale_set", "x_hi_set", "x_lo_set"))
        conv_done = sem("conv_done")
        y_set = sem("y_set")
        y_hi_set, y_lo_set = sem("y_hi_set"), sem("y_lo_set")
        lin_done = [sem(f"lin_done{c}") for c in range(3)]
        z_done = sem("z_done")
        z_open_set = sem("z_open_set")
        z_turn_done = sem("z_turn_done")
        z_hi_set, z_lo_set = sem("z_hi_set"), sem("z_lo_set")
        bias_set = sem("bias_set")
        res_set = sem("res_set")
        x_chain = sem("x_chain")
        unscale_set = sem("unscale_set")
        gate_chain = sem("gate_chain")

        block = ctx.enter_context(nc.Block())

        def bc(ap, axis, shape):
            return ap.unsqueeze(axis).broadcast_to(shape)

        def run_steps(eng, step):
            for t in range(2):
                step(t // 2, t, t % 2)
            with eng.Fori(1, TILES // 2 - 2) as i:
                for u in range(2):
                    step(i, i * 2 + u, u)
            for t in range(TILES - 4, TILES + 1):
                step(t // 2, t, t % 2)

        @block.sync
        def _(sp):
            def load_x(t, u):
                if later(t, 2):
                    sp.wait_ge(x_lo_set, t - 1)
                sp.dma_start(xc[:, u], x_cols[t]).then_inc(xc_in[u], 16)

            def load_res(t, u):
                if isinstance(t, int) and t == 1:
                    sp.wait_ge(w_lo_set, BLOCKS + 1)
                if later(t, 2):
                    sp.wait_ge(stored[u], uses(t - 2, u))
                sp.dma_start(res[:, u], x_rows[t]).then_inc(xr_in[u], 16)

            def load_toep(t, u):
                if u == 0:
                    sp.wait_ge(k_out, (t + 2) * (8 * HT))
                if later(t, 2):
                    sp.wait_ge(conv_done, 2 * t - 2)
                src = bass.AP(scratch.tensor, t * (HT * 2 * KROW) + 1, [[1, P], [KROW, 2 * HT], [1, LENGTH]])
                sp.dma_start(toep[:, u].rearrange("p s h n -> p (s h) n"), src).then_inc(toep_in[u], 16)

            def store_kernels(g):
                at = [g * (QUADS * 2 * HT * KROW) + (j * KROW + P) for j in range(HT)]
                if not isinstance(g, int):
                    at = [sp.snap(a) for a in at]
                sp.wait_ge(k_split, g + 1)
                for j in range(HT):
                    dst = bass.AP(scratch.tensor, at[j], [[STEP, STEP], [HT * KROW, 2 * QUADS], [1, STEP]])
                    src = k_parts[STEP * j:STEP * (j + 1)].rearrange("p q s c -> p (q s) c")
                    sp.dma_start(dst, src).then_inc(k_out, 16)

            def store(t, u):
                sp.wait_ge(res_set, 3 * t + 3)
                sp.dma_start(out[t], res[:, u]).then_inc(stored[u], 16)

            def load_w(k):
                if k >= BLOCKS:
                    sp.dma_start(res[:, 1], lora_b).then_inc(w_in[k // 2], 16)
                else:
                    if k >= RAW:
                        sp.wait_ge(w_lo_set, k + 2 - RAW)
                    sp.dma_start(w_raw[:, k % RAW:k % RAW + 2], weights[k:k + 2].rearrange("k p c -> p k c"))\
                        .then_inc(w_in[k // 2], 16)

            sp.dma_start(rate[:], rates).then_inc(params_in, 16)
            sp.dma_start(coef[:], coefs).then_inc(params_in, 16)
            load_x(0, 0)
            load_w(0)
            sp.wait_ge(skip_zeroed, 1)
            for j in range(HT):
                sp.dma_start(skip_q[STEP * j:STEP * j + 1, :], skip[j:j + 1, :]).then_inc(skip_in, 16)
            sp.wait_ge(consts_set, 1)
            sp.dma_start(bass.AP(scratch.tensor, 0, [[KROW, 2 * FEATURES], [1, P]]), zeros[:]).then_inc(pad_out, 16)
            load_w(2)
            load_w(4)
            load_x(1, 1)
            load_w(6)
            sp.dma_start(len_i[:], lengths.partition_broadcast(P)).then_inc(len_in, 16)
            load_w(BLOCKS)
            sp.dma_start(bias_all[:], bias.partition_broadcast(P)).then_inc(bias_in, 16)
            sp.dma_start(gate_bias[:], gate_b.partition_broadcast(P)).then_inc(bias_in, 16)
            store_kernels(0)
            sp.wait_ge(k_out, 16 * HT)
            sp.wait_ge(pad_out, 16)
            for h in range(HT):
                src = bass.AP(scratch.tensor, h * KROW + 1, [[1, P], [HT * KROW, 2], [1, LENGTH]])
                sp.dma_start(toep[:, 0, :, h], src).then_inc(toep_first[h], 16)

            def step(i, t, u):
                if known(t + 2, TILES):
                    load_x(t + 2, u)
                if known(t + 1, TILES):
                    load_toep(t + 1, 1 - u)
                if known(t, TILES):
                    load_res(t, u)
                if u == 0 and known(i + 1, GROUPS):
                    store_kernels(i + 1)
                if later(t, 1):
                    store(t - 1, 1 - u)

            run_steps(sp, step)
            for u in range(2):
                sp.wait_ge(stored[u], uses(TILES - 2 + u, u))

        @block.gpsimd
        def _(pool):
            pool.memset(skip_q[:], 0.0).then_inc(skip_zeroed, 1)
            pool.iota(ramp_i[:], [[1, STEP]], base=0, channel_multiplier=0).then_inc(pool_chain, 1)
            pool.iota(pos_i[:], [[P, BLOCKS]], base=0, channel_multiplier=1).then_inc(pool_chain, 1)
            pool.memset(swap[:], 0.0).then_inc(pool_chain, 1)
            pool.memset(ident[:], 0.0).then_inc(pool_chain, 1)
            pool.wait_ge(pool_chain, 4)
            pool.tensor_copy(ramp[:], ramp_i[:]).then_inc(pool_chain, 1)
            pool.tensor_copy(pos_f[:], pos_i[:]).then_inc(pool_chain, 1)
            pool.affine_select(out=swap[:], in_=swap[:], compare_op=ALU.not_equal, fill=1.0, base=WAVES,
                               pattern=[[-1, P]], channel_multiplier=1).then_inc(pool_chain, 1)
            pool.affine_select(out=ident[:], in_=ident[:], compare_op=ALU.not_equal, fill=1.0, base=0,
                               pattern=[[-1, P]], channel_multiplier=1).then_inc(pool_chain, 1)
            pool.wait_ge(pool_chain, 8)
            pool.affine_select(out=swap[:], in_=swap[:], compare_op=ALU.not_equal, fill=-1.0, base=-WAVES,
                               pattern=[[-1, P]], channel_multiplier=1).then_inc(pool_chain, 1)
            pool.memset(zeros[:], 0.0).then_inc(pool_chain, 1)
            pool.memset(ones[:], 1.0).then_inc(pool_chain, 1)
            pool.memset(before[:, 0:1], -3.0e38).then_inc(pool_chain, 1)
            pool.wait_ge(pool_chain, 12)
            pool.engine_nop().then_inc(consts_set, 1)

            def multiply_ramp(g):
                cols = slice(g * HG, g * HG + HG) if isinstance(g, int) else bass.ds(g * HG, HG)
                if later(g, 1):
                    pool.wait_ge(k_summed, g)
                    pool.wait_ge(wave_set, g)
                for rates_of, table, done in ((decay, wave, damp_arg_set), (turns, phase, phase_set)):
                    if isinstance(g, int) and g == 0:
                        pool.wait_ge(rates_set if table is wave else turns_set, 1)
                    for s in range(2):
                        ins = pool.tensor_tensor(table[:, s], bc(rates_of[:, s, cols], 2, [P, HG, STEP]),
                                                 bc(ramp[:], 1, [P, HG, STEP]), ALU.mult)
                    ins.then_inc(done, 1)

            def split_y(t, u):
                pool.wait_ge(y_hi_set, t + 1)
                if later(t, 2):
                    pool.wait_ge(lin_done[1], t - 1)
                pool.tensor_tensor(y_lo[:, u], y[:].rearrange("p i h b -> p i (h b)"), y_hi[:, u].bitcast(F32),
                                   ALU.subtract).then_inc(y_lo_set, 1)

            def add_bias(t, u):
                pool.wait_ge(xr_in[u], uses(t, u))
                pool.tensor_tensor(res[:, u], res[:, u], bias_all[:], ALU.add).then_inc(bias_set, 1)

            multiply_ramp(0)
            for k in range(BLOCKS + 1):
                if k == W_BEFORE_GROUP_1:
                    multiply_ramp(1)
                pool.wait_ge(w_hi_set, k + 1)
                if k < BLOCKS:
                    lo, raw, hi = w_lo[:, k], w_raw[:, k % RAW], w_hi[:, k]
                else:
                    lo, raw, hi = b_lo[:], res[:, 1], b_hi[:]
                pool.tensor_tensor(lo, raw, hi.bitcast(F32), ALU.subtract).then_inc(w_lo_set, 1)
            pool.wait_ge(bias_in, 32)

            def step(i, t, u):
                if u == 1 and known(i + 2, GROUPS):
                    multiply_ramp(i + 2)
                if known(t, TILES):
                    split_y(t, u)
                    add_bias(t, u)

            run_steps(pool, step)

        @block.scalar
        def _(act):
            def damp_waves(g):
                act.wait_ge(damp_arg_set, g + 1)
                act.activation(wave[:], wave[:], ACT.Exp).then_inc(damp_set, 1)

            def turn_waves(g):
                act.wait_ge(wrapped_set, g + 1)
                act.activation(phase[:], phase[:], ACT.Sin, bias=quarter_rad[:], scale=-TURN).then_inc(trig_set, 1)

            def split_x(t, u):
                act.wait_ge(x_scale_set, t + 1)
                if later(t, 2):
                    act.wait_ge(conv_done, 2 * t - 2)
                act.activation(x_hi[:, u], xc[:, u].rearrange("p h i b -> p h (i b)"), ACT.Copy,
                               scale=x_scale[:, u:u + 1]).then_inc(x_hi_set, 1)

            def split_w(k):
                act.wait_ge(w_in[k // 2], 16)
                hi, raw = (w_hi[:, k], w_raw[:, k % RAW]) if k < BLOCKS else (b_hi[:], res[:, 1])
                act.activation(hi, raw, ACT.Copy).then_inc(w_hi_set, 1)

            def split_y(t, u):
                act.wait_ge(y_set, 2 * t + 2)
                if later(t, 2):
                    act.wait_ge(lin_done[1], t - 1)
                act.activation(y_hi[:, u], y[:].rearrange("p i h b -> p i (h b)"), ACT.Copy).then_inc(y_hi_set, 1)

            def split_z(t):
                act.wait_ge(z_turn_done, t + 1)
                if later(t, 1):
                    act.wait_ge(lin_done[1], t)
                act.activation(z_parts[:], z_turned[:, 0:P], ACT.Copy).then_inc(z_hi_set, 1)

            act.wait_ge(rates_set, 1)
            act.activation(sm["tanh"][:], decay[:, 0], ACT.Tanh, scale=0.5).then_inc(half_set, 1)
            damp_waves(0)
            act.wait_ge(turns_set, 1)
            act.activation(sm["sin"][:], turns[:, 0], ACT.Sin, scale=0.5 * TURN).then_inc(half_set, 1)
            act.activation(sm["cos"][:], turns[:, 0], ACT.Sin, bias=quarter_all[:], scale=0.5 * TURN)\
                .then_inc(half_set, 1)
            turn_waves(0)
            for k in range(BLOCKS + 1):
                if k == W_BEFORE_GROUP_1:
                    split_x(0, 0)
                    damp_waves(1)
                    turn_waves(1)
                split_w(k)

            def step(i, t, u):
                if u == 1 and known(i + 2, GROUPS):
                    damp_waves(i + 2)
                if known(t, TILES):
                    split_y(t, u)
                if u == 1 and known(i + 2, GROUPS):
                    turn_waves(i + 2)
                if known(t + 1, TILES):
                    split_x(t + 1, 1 - u)
                if later(t, 1):
                    split_z(t - 1)

            run_steps(act, step)

        @block.tensor
        def _(pe):
            def swap_waves(g):
                pe.wait_ge(wave_set, g + 1)
                pe.matmul(swapped[:, 0:HG * STEP], swap[:], wave[:, 1], start=True, stop=True).then_inc(swap_done, 1)

            def sum_waves(g):
                pe.wait_ge(mode_set, g + 1)
                if later(g, 1):
                    pe.wait_ge(k_split, g)
                for q in range(QUADS):
                    mm = pe.matmul(k_sum[:, q], mode[:, HT * q:HT * q + HT], wave[:, 0, HT * q:HT * q + HT],
                                   start=True, stop=True)
                mm.then_inc(k_summed, 1)

            def sum_tops(t, u):
                pe.wait_ge(x_top_set, t + 1)
                pe.matmul(x_sum[:, u:u + 1], ones[:], x_top[:, u:u + 1], start=True, stop=True).then_inc(x_sum_done, 1)

            def convolve(t, u):
                if not isinstance(t, int) or t > 0:
                    pe.wait_ge(toep_in[u], uses(t, u) - 16 * (1 - u))
                for h in range(HT):
                    if isinstance(t, int) and t == 0:
                        pe.wait_ge(toep_first[h], 16)
                    if h % 2 == 0 and later(t, 1):
                        pe.wait_ge(y_set, 2 * t - 1 + h // 2)
                    for d in range(BLOCKS):
                        n = (BLOCKS - d) * BATCH
                        for part, x in ((0, x_hi), (0, x_lo), (1, x_hi)):
                            mm = pe.matmul(conv[h // 2][:, h % 2, d:BLOCKS], toep[:, u, part, h, d * P:(d + 1) * P],
                                           x[:, u, h, 0:n], start=(d == 0 and part == 0 and x is x_hi),
                                           stop=(d == BLOCKS - 1 and part == 1))
                    if h % 2 == 1:
                        mm.then_inc(conv_done, 1)

            def linear(t, u):
                pe.wait_ge(y_lo_set, t + 1)
                for n, c in enumerate((2, 0, 1)):
                    if later(t, 1):
                        pe.wait_ge(res_set, 3 * t - 2 + n)
                    for k in range(BLOCKS):
                        if isinstance(t, int) and t == 0 and c == 2:
                            pe.wait_ge(w_lo_set, k + 1)
                        for first, second in ((y_hi, w_hi), (y_hi, w_lo), (y_lo, w_hi)):
                            mm = pe.matmul(lin[c][:, 0:CH], first[:, u, k], second[:, k, c * CH:(c + 1) * CH],
                                           start=(k == 0 and first is y_hi and second is w_hi),
                                           stop=(k == BLOCKS - 1 and first is y_lo))
                    if c == 2:
                        mm.then_inc(z_done, 1)
                    if c == 0:
                        pe.wait_ge(z_open_set, t + 1)
                        if later(t, 1):
                            pe.wait_ge(z_lo_set, t)
                        pe.transpose(z_turned[:, 0:P], z_open[:], ident[:]).then_inc(z_turn_done, 1)
                if isinstance(t, int) and t == 0:
                    pe.wait_ge(w_lo_set, BLOCKS + 1)
                pe.wait_ge(z_lo_set, t + 1)
                for c in (2, 0, 1):
                    w = Z0 if c == 2 else CH
                    for rows, b in ((P, b_hi), (RMAX, b_lo)):
                        mm = pe.matmul(lin[c][:, 0:w], z_parts[0:rows], b[0:rows, c * CH:c * CH + w],
                                       start=False, stop=True, skip_group_check=True)
                    mm.then_inc(lin_done[c], 1)

            pe.wait_ge(consts_set, 1)
            sum_tops(0, 0)
            swap_waves(0)
            pe.wait_ge(sizes_set, 1)
            pe.matmul(k_sum[:].rearrange("p q h c -> p (q h c)")[:, 0:FEATURES], ones[:], k_sizes[:],
                      start=True, stop=True).then_inc(bound_done, 1)
            sum_waves(0)

            def step(i, t, u):
                if known(t, TILES):
                    pe.wait_ge(x_lo_set, t + 1)
                    if u == 0 and known(i + 1, GROUPS):
                        swap_waves(i + 1)
                    convolve(t, u)
                if u == 0 and known(i + 1, GROUPS):
                    sum_waves(i + 1)
                if known(t + 1, TILES):
                    sum_tops(t + 1, 1 - u)
                if later(t, 1):
                    linear(t - 1, 1 - u)

            run_steps(pe, step)

        @block.vector
        def _(dve):
            chained = [0]

            def link(ins):
                ins.then_inc(dve_chain, 1)
                chained[0] += 1

            def settle():
                dve.wait_ge(dve_chain, chained[0])

            for tile, upper, lower in ((quarter, 0.25, 0.0), (quarter_rad, 0.25 * TURN, 0.0), (twice_sign, 2.0, -2.0)):
                link(dve.memset(tile[0:WAVES], upper))
                link(dve.memset(tile[WAVES:P], lower))
            link(dve.memset(quarter_all[:], 0.25 * TURN))
            dve.wait_ge(params_in, 32)
            arg = rate[:, 0:2]
            link(dve.tensor_scalar(ex["k"][:], arg, LOG2E, MAGIC, ALU.mult, ALU.add))
            settle()
            link(dve.tensor_scalar(ex["k"][:], ex["k"][:], MAGIC, None, ALU.subtract))
            settle()
            link(dve.scalar_tensor_tensor(out=ex["r"][:], in0=ex["k"][:], scalar=-LN2_HI, in1=arg, op0=ALU.mult, op1=ALU.add))
            settle()
            link(dve.scalar_tensor_tensor(out=ex["r"][:], in0=ex["k"][:], scalar=-LN2_LO, in1=ex["r"][:],
                                          op0=ALU.mult, op1=ALU.add))
            link(dve.tensor_scalar(ex["k"][:], ex["k"][:], 126.0, -126.0, ALU.min, ALU.max))
            settle()
            link(dve.tensor_scalar(ex_bits[:], ex["k"][:], 127.0, float(1 << 23), ALU.add, ALU.mult))
            link(dve.tensor_scalar(ex["p"][:], ex["r"][:], 1.0 / math.factorial(7), None, ALU.mult))
            for n in range(6, 0, -1):
                settle()
                link(dve.scalar_tensor_tensor(out=ex["p"][:], in0=ex["p"][:], scalar=1.0 / math.factorial(n),
                                              in1=ex["r"][:], op0=ALU.add, op1=ALU.mult))
            settle()
            link(dve.scalar_tensor_tensor(out=ex["e"][:], in0=ex["p"][:], scalar=1.0, in1=ex_bits[:].bitcast(F32),
                                          op0=ALU.add, op1=ALU.mult))
            settle()
            dt, ar, ai = ex["e"][:, 0], ex["e"][:, 1], rate[:, 2]
            link(dve.scalar_tensor_tensor(out=decay[:, 0], in0=ar, scalar=-1.0, in1=dt, op0=ALU.mult, op1=ALU.mult))
            link(dve.tensor_tensor(theta[:, 0], ai, dt, ALU.mult))
            settle()
            link(dve.tensor_scalar(theta[:, 1], theta[:, 0], float(STEP), None, ALU.mult))
            dve.tensor_scalar(decay[:, 1], decay[:, 0], float(STEP), None, ALU.mult).then_inc(rates_set, 1)
            settle()
            link(dve.tensor_scalar(th_k[:], theta[:], 1.0 / (2 * math.pi), MAGIC, ALU.mult, ALU.add))
            settle()
            link(dve.tensor_scalar(th_k[:], th_k[:], MAGIC, None, ALU.subtract))
            for part in (PI2_HI, PI2_MID, PI2_LO):
                settle()
                link(dve.scalar_tensor_tensor(out=theta[:], in0=th_k[:], scalar=-part, in1=theta[:],
                                              op0=ALU.mult, op1=ALU.add))
            settle()
            dve.tensor_scalar(turns[:], theta[:], 1.0 / (2 * math.pi), None, ALU.mult).then_inc(turns_set, 1)
            dve.wait_ge(turns_set, 1)
            dve.wait_ge(consts_set, 1)

            def wrap_phases(g):
                dve.wait_ge(phase_set, g + 1)
                if later(g, 1):
                    dve.wait_ge(wrapped_set, g)
                dve.tensor_scalar(whole[:], phase[:], quarter[:], MAGIC, ALU.add, ALU.add).then_inc(whole_set, 1)
                dve.wait_ge(whole_set, g + 1)
                dve.scalar_tensor_tensor(out=phase[:], in0=whole[:], scalar=MAGIC, in1=phase[:],
                                         op0=ALU.subtract, op1=ALU.subtract).then_inc(wrapped_set, 1)

            def finish_waves(g):
                dve.wait_ge(damp_set, g + 1)
                dve.wait_ge(trig_set, g + 1)
                dve.tensor_tensor(wave[:], wave[:], phase[:], ALU.mult).then_inc(wave_set, 1)

            def weigh_waves(g):
                cols = slice(g * HG, g * HG + HG) if isinstance(g, int) else bass.ds(g * HG, HG)
                dve.wait_ge(wave_set, g + 1)
                if later(g, 1):
                    dve.wait_ge(k_summed, g)
                tt(mode_re[:], wave[:, 1], bc(sm["gre"][:, cols], 2, [P, HG, STEP]), ALU.mult).then_inc(mode_chain, 1)
                dve.wait_ge(swap_done, g + 1)
                tt(mode_im[:], swapped[:, 0:HG * STEP].rearrange("p (h a) -> p h a", h=HG),
                   bc(sm["gim"][:, cols], 2, [P, HG, STEP]), ALU.mult).then_inc(mode_chain, 1)
                dve.wait_ge(mode_chain, 2 * g + 2)
                tt(mode[:], mode_re[:], mode_im[:], ALU.add).then_inc(mode_set, 1)

            def take_kernels(g):
                dve.wait_ge(k_summed, g + 1)
                if later(g, 1):
                    dve.wait_ge(k_split, g)
                    dve.wait_ge(k_out, g * (16 * HT))
                for j in range(HT):
                    dve.tensor_copy(kern[STEP * j:STEP * (j + 1)], k_sum[STEP * j:STEP * (j + 1), :, j])\
                        .then_inc(kern_chain, 1)
                dve.wait_ge(kern_chain, 6 * g + 4)
                quads = slice(g * QUADS, g * QUADS + QUADS) if isinstance(g, int) else bass.ds(g * QUADS, QUADS)
                tt(kern[:, :, 0], kern[:, :, 0], skip_q[:, quads], ALU.add).then_inc(kern_chain, 1)
                dve.wait_ge(kern_chain, 6 * g + 5)
                dve.tensor_copy(k_parts[:, :, 0], kern[:]).then_inc(kern_chain, 1)
                dve.wait_ge(kern_chain, 6 * g + 6)
                tt(k_parts[:, :, 1], kern[:], k_parts[:, :, 0], ALU.subtract).then_inc(k_split, 1)

            def top_x(t, u):
                dve.wait_ge(xc_in[u], uses(t, u))
                dve.tensor_reduce(x_top[:, u:u + 1], xc[:, u].rearrange("p h i b -> p (h i b)"), AX.X, ALU.max,
                                  apply_absolute_value=True).then_inc(x_top_set, 1)

            def scale_x(t, u):
                dve.wait_ge(x_sum_done, t + 1)
                dve.tensor_scalar(x_pow[:, u:u + 1], x_sum[:, u:u + 1], 2.0**-60, None, ALU.max).then_inc(x_chain, 1)
                dve.wait_ge(x_chain, 3 * t + 1)
                dve.tensor_scalar(x_pow[:, u:u + 1].bitcast(I32), x_pow[:, u:u + 1].bitcast(I32), EXPONENT_BITS, None,
                                  ALU.bitwise_and).then_inc(x_chain, 1)
                dve.wait_ge(x_chain, 3 * t + 2)
                dve.reciprocal(x_rec[:, u:u + 1], x_pow[:, u:u + 1]).then_inc(x_chain, 1)
                dve.wait_ge(x_chain, 3 * t + 3)
                dve.tensor_scalar(x_scale[:, u:u + 1], x_rec[:, u:u + 1], 2.0**14, None, ALU.mult)\
                    .then_inc(x_scale_set, 1)

            def split_x(t, u):
                dve.wait_ge(x_hi_set, t + 1)
                dve.scalar_tensor_tensor(
                    out=x_lo[:, u].rearrange("p h n -> p (h n)"), in0=xc[:, u].rearrange("p h i b -> p (h i b)"),
                    scalar=x_scale[:, u:u + 1], in1=x_hi[:, u].rearrange("p h n -> p (h n)"), op0=ALU.mult,
                    op1=ALU.subtract).then_inc(x_lo_set, 1)

            s = {n: v[:] for n, v in sm.items()}
            tt = dve.tensor_tensor

            def stt(o, a, scalar, b, op0, op1):
                return dve.scalar_tensor_tensor(out=o, in0=a, scalar=scalar, in1=b, op0=op0, op1=op1)

            wrap_phases(0)
            top_x(0, 0)
            dve.wait_ge(half_set, 3)
            link(dve.tensor_scalar(s["den"], s["tanh"], -1.0, 1.0, ALU.mult, ALU.add))
            link(tt(s["n1"], s["sin"], s["sin"], ALU.mult))
            link(tt(s["n2"], s["sin"], s["cos"], ALU.mult))
            link(tt(s["n3"], ar, ar, ALU.mult))
            link(tt(s["n4"], ai, ai, ALU.mult))
            settle()
            link(dve.reciprocal(s["den"], s["den"]))
            link(tt(s["rabs2"], s["n3"], s["n4"], ALU.add))
            settle()
            link(stt(s["em"], s["tanh"], 2.0, s["den"], ALU.mult, ALU.mult))
            link(dve.reciprocal(s["rabs2"], s["rabs2"]))
            settle()
            link(stt(s["n3"], s["em"], 1.0, s["n1"], ALU.add, ALU.mult))
            link(stt(s["n4"], s["em"], 1.0, s["n2"], ALU.add, ALU.mult))
            settle()
            link(stt(s["zre"], s["n3"], -2.0, s["em"], ALU.mult, ALU.add))
            link(dve.tensor_scalar(s["zim"], s["n4"], 2.0, None, ALU.mult))
            settle()
            link(tt(s["n1"], ar, s["zre"], ALU.mult))
            link(tt(s["n2"], ai, s["zim"], ALU.mult))
            link(stt(s["n3"], s["zim"], -1.0, ar, ALU.mult, ALU.mult))
            link(tt(s["n4"], ai, s["zre"], ALU.mult))
            settle()
            link(tt(s["nre"], s["n2"], s["n1"], ALU.subtract))
            link(tt(s["nim"], s["n3"], s["n4"], ALU.subtract))
            settle()
            cre, cim = coef[:, 0], coef[:, 1]
            link(tt(s["n1"], cre, s["nre"], ALU.mult))
            link(tt(s["n2"], cim, s["nim"], ALU.mult))
            link(tt(s["n3"], cre, s["nim"], ALU.mult))
            link(tt(s["n4"], cim, s["nre"], ALU.mult))
            settle()
            link(tt(s["zre"], s["n1"], s["n2"], ALU.subtract))
            link(tt(s["zim"], s["n3"], s["n4"], ALU.add))
            settle()
            link(stt(s["gre"], s["zre"], twice_sign[:], s["rabs2"], ALU.mult, ALU.mult))
            link(stt(s["gim"], s["zim"], twice_sign[:], s["rabs2"], ALU.mult, ALU.mult))
            settle()
            link(stt(s["n1"], s["gre"], -1.0, s["gre"], ALU.mult, ALU.max))
            link(stt(s["n2"], s["gim"], -1.0, s["gim"], ALU.mult, ALU.max))
            settle()
            tt(k_sizes[:], s["n1"], s["n2"], ALU.add).then_inc(sizes_set, 1)
            link(stt(s["n3"], rate[:, 3], -1.0, rate[:, 3], ALU.mult, ALU.max))
            finish_waves(0)
            settle()
            dve.wait_ge(bound_done, 1)
            link(tt(k_bound[:], k_sum[:].rearrange("p q h c -> p (q h c)")[:, 0:FEATURES], s["n3"], ALU.add))
            settle()
            link(dve.tensor_reduce(k_pow[:], k_bound[:].rearrange("p (t h) -> p t h", h=HT), AX.X, ALU.max))
            settle()
            link(dve.tensor_scalar(k_pow[:], k_pow[:], 2.0**-60, None, ALU.max))
            settle()
            link(dve.tensor_scalar(k_pow[:].bitcast(I32), k_pow[:].bitcast(I32), EXPONENT_BITS, None, ALU.bitwise_and))
            settle()
            link(dve.reciprocal(k_scale[:], k_pow[:]))
            settle()
            link(dve.tensor_scalar(k_scale[:], k_scale[:], 2.0**14, None, ALU.mult))
            settle()
            by_tile = bc(k_scale[:], 2, [P, TILES, HT])
            for g_part in (s["gre"], s["gim"]):
                view = g_part.rearrange("p (t h) -> p t h", h=HT)
                link(tt(view, view, by_tile, ALU.mult))
            dve.wait_ge(skip_in, 16 * HT)
            link(tt(skip_q[:], skip_q[:], k_scale[:], ALU.mult))
            settle()
            weigh_waves(0)
            scale_x(0, 0)
            take_kernels(0)
            split_x(0, 0)
            top_x(1, 1)

            dve.wait_ge(len_in, 16)
            link(dve.tensor_copy(len_f[:], len_i[:]))
            settle()
            link(tt(mask[:], bc(pos_f[:], 2, [P, BLOCKS, BATCH]), bc(len_f[:], 1, [P, BLOCKS, BATCH]), ALU.is_lt))
            settle()
            wrap_phases(1)
            finish_waves(1)
            dve.wait_ge(bias_in, 32)

            def take_y(t, u, n):
                if n == 0:
                    stt(unscale[:, u:u + 1], x_pow[:, u:u + 1], 2.0**-28, k_pow[:, bass.ds(t, 1)], ALU.mult, ALU.mult)\
                        .then_inc(unscale_set, 1)
                    dve.wait_ge(unscale_set, t + 1)
                    if later(t, 1):
                        dve.wait_ge(y_lo_set, t)
                dve.wait_ge(conv_done, 2 * t + n + 1)
                for h in range(2):
                    ins = stt(y[:, :, 2 * n + h], conv[n][:, h], unscale[:, u:u + 1], mask[:], ALU.mult, ALU.mult)
                ins.then_inc(y_set, 1)

            def pick_rank(t):
                z = lin[2][:, Z0:Z0 + RMAX]
                dve.wait_ge(z_done, t + 1)
                tt(score[:], lin[2][:, Z0 + RMAX:Z0 + RMAX + 4], gate_bias[:], ALU.add).then_inc(gate_chain, 1)
                dve.wait_ge(gate_chain, 4 * t + 1)
                dve.tensor_reduce(best[:], score[:], AX.X, ALU.max)
                dve.tensor_copy(before[:, 1:2], score[:, 0:1])
                tt(before[:, 2:4], score[:, 0:1].broadcast_to([P, 2]), score[:, 1:2].broadcast_to([P, 2]), ALU.max)\
                    .then_inc(gate_chain, 1)
                dve.wait_ge(gate_chain, 4 * t + 2)
                tt(before[:, 4:8], before[:, 2:3].broadcast_to([P, 4]), score[:, 2:3].broadcast_to([P, 4]), ALU.max)\
                    .then_inc(gate_chain, 1)
                dve.wait_ge(gate_chain, 4 * t + 3)
                dve.tensor_scalar(open8[:], before[:], best[:], None, ALU.is_lt).then_inc(gate_chain, 1)
                dve.wait_ge(gate_chain, 4 * t + 4)
                if later(t, 1):
                    dve.wait_ge(z_turn_done, t)
                for twice in range(2):
                    ins = tt(z_open[:, twice].rearrange("p (g c) -> p g c", g=8), z.rearrange("p (g c) -> p g c", g=8),
                             bc(open8[:], 2, [P, 8, 8]), ALU.mult)
                ins.then_inc(z_open_set, 1)

            def split_z(t):
                dve.wait_ge(z_hi_set, t + 1)
                tt(z_parts[RMAX:P], z_turned[RMAX:P, 0:P], z_parts[RMAX:P].bitcast(F32), ALU.subtract)\
                    .then_inc(z_lo_set, 1)

            def finish(t, u):
                dve.wait_ge(bias_set, t + 1)
                for c in (2, 0, 1):
                    w = Z0 if c == 2 else CH
                    dve.wait_ge(lin_done[c], t + 1)
                    tt(res[:, u, c * CH:c * CH + w], res[:, u, c * CH:c * CH + w], lin[c][:, 0:w], ALU.add)\
                        .then_inc(res_set, 1)

            def step(i, t, u):
                if u == 0 and known(i + 1, GROUPS):
                    weigh_waves(i + 1)
                if known(t + 1, TILES) and later(t, 1):
                    top_x(t + 1, 1 - u)
                if u == 1 and known(i + 2, GROUPS):
                    wrap_phases(i + 2)
                if known(t, TILES):
                    take_y(t, u, 0)
                    take_y(t, u, 1)
                if u == 0 and known(i + 1, GROUPS):
                    take_kernels(i + 1)
                if known(t + 1, TILES):
                    scale_x(t + 1, 1 - u)
                if later(t, 1):
                    pick_rank(t - 1)
                if known(t + 1, TILES):
                    split_x(t + 1, 1 - u)
                if u == 1 and known(i + 2, GROUPS):
                    finish_waves(i + 2)
                if later(t, 1):
                    split_z(t - 1)
                    finish(t - 1, 1 - u)

            run_steps(dve, step)


def kernel(x, itok_B_8_3872, L0_cond_log_dt, L0_cond_C, L0_cond_log_A_real, L0_cond_A_imag, L0_cond_D,
           L0_ffn_W, L0_ffn_b, L0_ffn_A, L0_ffn_B, L0_ffn_gate_w, L0_ffn_gate_b):
    import concourse.bacc as bacc
    from concourse.bass_utils import run_bass_kernel_spmd

    def lay(a):
        return np.ascontiguousarray(a)

    x = np.asarray(x)
    x_rows = lay(x.transpose(1, 0, 2).reshape(TILES, P, LENGTH))
    x_cols = lay(x.reshape(BATCH, TILES, HT, BLOCKS, P)[..., ::-1].transpose(1, 4, 2, 3, 0))
    twice = lambda a: np.concatenate([a, a])
    log_dt = np.broadcast_to(np.asarray(L0_cond_log_dt), (WAVES, FEATURES))
    all_skip = np.broadcast_to(np.asarray(L0_cond_D), (WAVES, FEATURES))
    rates = lay(twice(np.stack([log_dt, np.asarray(L0_cond_log_A_real).T, np.asarray(L0_cond_A_imag).T, all_skip], 1)))
    coefs = lay(twice(np.asarray(L0_cond_C).transpose(1, 2, 0)))
    skip = lay(np.asarray(L0_cond_D).reshape(TILES, HT).T)
    weights = lay(np.concatenate([np.asarray(a) for a in (L0_ffn_W, L0_ffn_A, L0_ffn_gate_w)]).T
                  .reshape(BLOCKS, P, COLS))
    lora_b = lay(twice(np.asarray(L0_ffn_B).T))

    nc = bacc.Bacc("TRN2", target_bir_lowering=False, num_devices=1)
    arrays = {
        "x_rows": x_rows, "x_cols": x_cols, "lengths": lay(itok_B_8_3872), "rates": rates, "coefs": coefs,
        "skip": skip, "weights": weights, "bias": lay(L0_ffn_b), "lora_b": lora_b, "gate_b": lay(L0_ffn_gate_b),
    }
    args = [nc.dram_tensor(n, a.shape, mybir.dt.from_np(a.dtype), kind="ExternalInput").ap() for n, a in arrays.items()]
    scratch = nc.dram_tensor("kernels", (TILES, 2, HT, KROW), F16, kind="Internal").ap()
    out = nc.dram_tensor("out", (TILES, P, LENGTH), F32, kind="ExternalOutput").ap()
    build(nc, *args, scratch, out)
    r = run_bass_kernel_spmd(nc, [arrays], core_ids=[0])
    return r.results[0]["out"].reshape(FEATURES, BATCH, LENGTH).transpose(1, 0, 2)
```

```python
import math
from contextlib import ExitStack

import numpy as np

import concourse.bass as bass
from concourse import mybir
from concourse.alu_op_type import AluOpType as ALU

F32 = mybir.dt.float32
F32R = mybir.dt.float32r
F16 = mybir.dt.float16
BF16 = mybir.dt.bfloat16
I32 = mybir.dt.int32
ACT = mybir.ActivationFunctionType
AX = mybir.AxisListType

P = 128
BATCH, FEATURES, LENGTH = 32, 64, 1024
WAVES = 64
BLOCKS = LENGTH // P
HT = P // BATCH
TILES = FEATURES // HT
HG = 8
GROUPS = FEATURES // HG
QUADS = HG // HT
STEP = 32
RANKS = (8, 16, 32, 64)
RMAX = RANKS[-1]
COLS = LENGTH + RMAX + len(RANKS)
CH = COLS // 3
Z0 = LENGTH - 2 * CH
KROW = P + LENGTH
LENT = 4
WARM_UP = 8
W_POOL = 6

MAGIC = 12582912.0
LOG2E = 1.0 / math.log(2.0)
LN2_HI = 0.693359375
LN2_LO = math.log(2.0) - LN2_HI
PI2_HI = 6.28125
PI2_MID = float(np.round((2 * math.pi - PI2_HI) * 2**20) / 2**20)
PI2_LO = 2 * math.pi - PI2_HI - PI2_MID
TURN = float(np.nextafter(np.float32(2 * math.pi), np.float32(0)))
EXPONENT_BITS = 0x7F800000


def later(t, n):
    return not isinstance(t, int) or t >= n


def known(n, below):
    return not isinstance(n, int) or 0 <= n < below


def uses(t, u):
    return (t - u) * 8 + 16


def build(nc, x_rows, x_cols, lengths, rates, coefs, skip, weights, bias, lora_b, gate_b, scratch, out):
    with ExitStack() as ctx:
        def sb(name, shape, dt=F32):
            return ctx.enter_context(nc.sbuf_tensor(name, shape, dt))

        def sem(name):
            return ctx.enter_context(nc.semaphore(name))

        swap = sb("swap", [P, P])
        ident = sb("ident", [P, P])
        ramp_i = sb("ramp_i", [P, STEP], I32)
        ramp = sb("ramp", [P, STEP])
        quarter = sb("quarter", [P, 1])
        quarter_rad = sb("quarter_rad", [P, 1])
        quarter_all = sb("quarter_all", [P, 1])
        twice_sign = sb("twice_sign", [P, 1])
        rate = sb("rate", [P, 4, FEATURES])
        coef = sb("coef", [P, 2, FEATURES])
        skip_q = sb("skip_q", [P, TILES])
        ones = sb("ones", [P, P], BF16)
        len_i = sb("len_i", [P, BATCH], I32)
        len_f = sb("len_f", [P, BATCH])
        pos_i = sb("pos_i", [P, BLOCKS], I32)
        pos_f = sb("pos_f", [P, BLOCKS])
        mask = sb("mask", [P, BLOCKS, BATCH])
        bias_all = sb("bias_all", [P, LENGTH])
        gate_bias = sb("gate_bias", [P, len(RANKS)])
        ex = {n: sb("ex_" + n, [P, 2, FEATURES]) for n in ("k", "r", "p", "e")}
        ex_bits = sb("ex_bits", [P, 2, FEATURES], I32)
        decay = sb("decay", [P, 2, FEATURES])
        theta = sb("theta", [P, 2, FEATURES])
        turns = sb("turns", [P, 2, FEATURES])
        th_k = sb("th_k", [P, 2, FEATURES])
        sm = {n: sb("sm_" + n, [P, FEATURES]) for n in (
            "tanh", "sin", "cos", "den", "em", "zre", "zim", "ar2", "ai2", "rabs2",
            "cre_ar", "cre_ai", "cim_ar", "cim_ai", "qre", "qim", "abs_skip", "n1", "n2", "n3", "n4", "gre", "gim")}
        phase = sb("phase", [P, 2, HG, STEP])
        whole = sb("whole", [P, 2, HG, STEP])
        wave = sb("wave", [P, 2, HG, STEP])
        swapped_sb = sb("swapped", [P, HG, STEP])
        mode_re = sb("mode_re", [P, HG, STEP])
        mode_im = sb("mode_im", [P, HG, STEP])
        mode = sb("mode", [P, HG, STEP])
        kern = sb("kern", [P, QUADS, STEP])
        k_sizes = sb("k_sizes", [P, FEATURES], BF16)
        k_bound = sb("k_bound", [P, FEATURES])
        k_pow = sb("k_pow", [P, TILES])
        k_scale = sb("k_scale", [P, TILES])
        k_parts = sb("k_parts", [P, QUADS, 2, STEP], F16)
        zeros = sb("zeros", [P, P], F16)
        w_late = sb("w_late", [P, BLOCKS - LENT, COLS])
        w_hi = sb("w_hi", [P, BLOCKS, COLS], F32R)
        w_lo = sb("w_lo", [P, BLOCKS, COLS], F32R)
        b_hi = sb("b_hi", [P, LENGTH], F32R)
        b_lo = sb("b_lo", [P, LENGTH], F32R)
        xc = sb("xc", [P, 2, HT, BLOCKS, BATCH])
        x_hi = sb("x_hi", [P, 2, HT, BLOCKS * BATCH], F16)
        x_lo = sb("x_lo", [P, 2, HT, BLOCKS * BATCH], F16)
        x_top = sb("x_top", [P, 2], BF16)
        x_pow = sb("x_pow", [P, 2])
        x_rec = sb("x_rec", [P, 2])
        x_scale = sb("x_scale", [P, 2])
        unscale = sb("unscale", [P, 2])
        toep = sb("toep", [P, 2, 2, HT, LENGTH], F16)
        y = sb("y", [P, BLOCKS, HT, BATCH])
        y_hi = sb("y_hi", [P, 2, BLOCKS, P], F32R)
        y_lo = sb("y_lo", [P, 2, BLOCKS, P], F32R)
        res = sb("res", [P, 2, LENGTH])
        score = sb("score", [P, 4])
        best = sb("best", [P, 1])
        before = sb("before", [P, 8])
        open8 = sb("open8", [P, 8])
        z_open = sb("z_open", [P, 2, RMAX])
        z_parts = sb("z_parts", [P, P], F32R)

        conv = [ctx.enter_context(nc.psum_tensor(f"conv{n}", [P, 2, BLOCKS, BATCH], F32)) for n in range(2)]
        lin = [ctx.enter_context(nc.psum_tensor(f"lin{n}", [P, 512], F32)) for n in range(3)]
        z_turned = ctx.enter_context(nc.psum_tensor("z_turned", [P, 512], F32))
        k_bound_sum = lin[1][:, 0:FEATURES]
        swapped_early = z_turned[:, P:P + HG * STEP].rearrange("p (h a) -> p h a", h=HG)
        x_sum = ctx.enter_context(nc.psum_tensor("x_sum", [P, 2], F32))
        k_sum = ctx.enter_context(nc.psum_tensor("k_sum", [P, QUADS, HT, STEP], F32))

        lent = toep[:].rearrange("p u s h n -> p u (s h n)").bitcast(F32)[:, :, 0:2 * COLS]\
            .rearrange("p u (k c) -> p u k c", k=2)
        w_raw = [lent[:, k // 2, k % 2] if k < LENT else w_late[:, k - LENT] for k in range(BLOCKS)] + [res[:, 1]]

        rates_in, coefs_in, skip_in, len_in, bias_in, gate_in = map(
            sem, ("rates_in", "coefs_in", "skip_in", "len_in", "bias_in", "gate_in"))
        w_in = [sem(f"w_in{k}") for k in range(0, BLOCKS + 1, 2)]
        xc_in = [sem("xc_in0"), sem("xc_in1")]
        xr_in = [sem("xr_in0"), sem("xr_in1")]
        toep_in = [sem("toep_in0"), sem("toep_in1")]
        stored = [sem("stored0"), sem("stored1")]
        pad_out = sem("pad_out")
        early = [[sem(f"early{t}_{h}") for h in range(HT)] for t in range(2)]
        k_out = sem("k_out")
        consts_set = sem("consts_set")
        skip_zeroed = sem("skip_zeroed")
        pool_chain = sem("pool_chain")
        dve_chain = sem("dve_chain")
        rates_set = sem("rates_set")
        turns_set = sem("turns_set")
        half_set = sem("half_set")
        damp_arg_set = sem("damp_arg_set")
        phase_set = sem("phase_set")
        damp_set = sem("damp_set")
        whole_set = sem("whole_set")
        wrapped_set = sem("wrapped_set")
        trig_set = sem("trig_set")
        wave_set = sem("wave_set")
        swap_done = sem("swap_done")
        swap_in = sem("swap_in")
        mode_chain = sem("mode_chain")
        mode_set = sem("mode_set")
        k_summed = sem("k_summed")
        kern_chain = sem("kern_chain")
        k_split = sem("k_split")
        sizes_set, bound_done = sem("sizes_set"), sem("bound_done")
        w_hi_set = sem("w_hi_set")
        w_lo_set = sem("w_lo_set")
        w_lo_late_set = sem("w_lo_late_set")
        x_top_set, x_sum_done, x_scale_set, x_hi_set, x_lo_set = map(
            sem, ("x_top_set", "x_sum_done", "x_scale_set", "x_hi_set", "x_lo_set"))
        conv_done = sem("conv_done")
        y_set = sem("y_set")
        y_hi_set, y_lo_set = sem("y_hi_set"), sem("y_lo_set")
        lin_done = [sem(f"lin_done{c}") for c in range(3)]
        z_done = sem("z_done")
        z_open_set = sem("z_open_set")
        z_turn_done = sem("z_turn_done")
        z_hi_set, z_lo_set = sem("z_hi_set"), sem("z_lo_set")
        bias_set = sem("bias_set")
        res_set = sem("res_set")
        x_chain = sem("x_chain")
        unscale_set = sem("unscale_set")
        gate_chain = sem("gate_chain")

        block = ctx.enter_context(nc.Block())

        def bc(ap, axis, shape):
            return ap.unsqueeze(axis).broadcast_to(shape)

        def run_steps(eng, step):
            for t in range(2):
                step(t // 2, t, t % 2)
            with eng.Fori(1, TILES // 2 - 2) as i:
                for u in range(2):
                    step(i, i * 2 + u, u)
            for t in range(TILES - 4, TILES + 1):
                step(t // 2, t, t % 2)

        @block.sync
        def _(sp):
            def load_x(t, u):
                if later(t, 2):
                    sp.wait_ge(x_lo_set, t - 1)
                sp.dma_start(xc[:, u], x_cols[t]).then_inc(xc_in[u], 16)

            def load_res(t, u):
                if isinstance(t, int) and t == 1:
                    sp.wait_ge(w_lo_set, W_POOL + 1)
                if later(t, 2):
                    sp.wait_ge(stored[u], uses(t - 2, u))
                sp.dma_start(res[:, u], x_rows[t]).then_inc(xr_in[u], 16)

            def load_toep(t, u):
                if u == 0:
                    sp.wait_ge(k_out, t * (8 * HT))
                sp.wait_ge(conv_done, 2 * t - 2)
                src = bass.AP(scratch.tensor, t * (HT * 2 * KROW) + 1, [[1, P], [KROW, 2 * HT], [1, LENGTH]])
                sp.dma_start(toep[:, u].rearrange("p s h n -> p (s h) n"), src).then_inc(toep_in[u], 16)

            def store_kernels(g):
                at = [g * (QUADS * 2 * HT * KROW) + (j * KROW + P) for j in range(HT)]
                if not isinstance(g, int):
                    at = [sp.snap(a) for a in at]
                sp.wait_ge(k_split, g + 1)
                for j in range(HT):
                    dst = bass.AP(scratch.tensor, at[j], [[STEP, STEP], [HT * KROW, 2 * QUADS], [1, STEP]])
                    src = k_parts[STEP * j:STEP * (j + 1)].rearrange("p q s c -> p (q s) c")
                    sp.dma_start(dst, src).then_inc(early[0][j] if isinstance(g, int) and g == 0 else k_out, 16)

            def swap_waves(g):
                sp.wait_ge(wave_set, g + 1)
                sp.dma_start(swapped_sb[0:WAVES], wave[WAVES:P, 1]).then_inc(swap_in, 16)
                sp.dma_start(swapped_sb[WAVES:P], wave[0:WAVES, 1]).then_inc(swap_in, 16)

            def store(t, u):
                if isinstance(t, int) and t == TILES - 1:
                    for n, c in enumerate((2, 0, 1)):
                        w = Z0 if c == 2 else CH
                        sp.wait_ge(res_set, 3 * t + 1 + n)
                        sp.dma_start(out[t, :, c * CH:c * CH + w], res[:, u, c * CH:c * CH + w]).then_inc(stored[u], 16)
                else:
                    sp.wait_ge(res_set, 3 * t + 3)
                    sp.dma_start(out[t], res[:, u]).then_inc(stored[u], 16)

            def load_w(k):
                if k >= BLOCKS:
                    sp.dma_start(w_raw[k], lora_b).then_inc(w_in[k // 2], 16)
                else:
                    dst = lent[:, k // 2] if k < LENT else w_late[:, k - LENT:k - LENT + 2]
                    sp.dma_start(dst, weights[k:k + 2].rearrange("k p c -> p k c")).then_inc(w_in[k // 2], 16)

            sp.dma_start(rate[:], rates).then_inc(rates_in, 16)
            sp.dma_start(coef[:], coefs).then_inc(coefs_in, 16)
            load_w(0)
            load_w(2)
            sp.wait_ge(skip_zeroed, 1)
            for j in range(HT):
                sp.dma_start(skip_q[STEP * j:STEP * j + 1, :], skip[j:j + 1, :]).then_inc(skip_in, 16)
            sp.wait_ge(consts_set, 1)
            sp.dma_start(bass.AP(scratch.tensor, 0, [[KROW, 2 * FEATURES], [1, P]]), zeros[:]).then_inc(pad_out, 16)
            load_x(0, 0)
            load_w(4)
            load_x(1, 1)
            load_w(6)
            load_w(BLOCKS)
            sp.dma_start(len_i[:], lengths.partition_broadcast(P)).then_inc(len_in, 16)
            sp.dma_start(gate_bias[:], gate_b.partition_broadcast(P)).then_inc(gate_in, 16)
            store_kernels(0)
            sp.wait_ge(pad_out, 16)
            for t in range(2):
                sp.wait_ge(w_lo_set, 2 * t + 2)
                for h in range(HT):
                    if t == 0:
                        sp.wait_ge(early[0][h], 16)
                    src = bass.AP(scratch.tensor, (2 * t * HT + h) * KROW + 1, [[1, P], [HT * KROW, 2], [1, LENGTH]])
                    sp.dma_start(toep[:, t, :, h], src).then_inc(early[t][h], 16)
            sp.dma_start(bias_all[:], bias.partition_broadcast(P)).then_inc(bias_in, 16)

            def step(i, t, u):
                if known(t + 2, TILES):
                    load_x(t + 2, u)
                if known(t + 1, TILES) and later(t, 1):
                    load_toep(t + 1, 1 - u)
                if known(t, TILES):
                    load_res(t, u)
                if u == 0 and known(i + 1, GROUPS):
                    store_kernels(i + 1)
                if later(t, 1):
                    store(t - 1, 1 - u)
                if u == 1 and known(i + 2, GROUPS):
                    swap_waves(i + 2)

            run_steps(sp, step)
            for u in range(2):
                sp.wait_ge(stored[u], uses(TILES - 2 + u, u) + 32 * u)

        @block.gpsimd
        def _(pool):
            pool.memset(skip_q[:], 0.0).then_inc(skip_zeroed, 1)
            pool.iota(ramp_i[:], [[1, STEP]], base=0, channel_multiplier=0).then_inc(pool_chain, 1)
            pool.iota(pos_i[:], [[P, BLOCKS]], base=0, channel_multiplier=1).then_inc(pool_chain, 1)
            pool.memset(swap[:], 0.0).then_inc(pool_chain, 1)
            pool.memset(ident[:], 0.0).then_inc(pool_chain, 1)
            pool.wait_ge(pool_chain, 4)
            pool.tensor_copy(ramp[:], ramp_i[:]).then_inc(pool_chain, 1)
            pool.tensor_copy(pos_f[:], pos_i[:]).then_inc(pool_chain, 1)
            pool.affine_select(out=swap[:], in_=swap[:], compare_op=ALU.not_equal, fill=1.0, base=WAVES,
                               pattern=[[-1, P]], channel_multiplier=1).then_inc(pool_chain, 1)
            pool.affine_select(out=ident[:], in_=ident[:], compare_op=ALU.not_equal, fill=1.0, base=0,
                               pattern=[[-1, P]], channel_multiplier=1).then_inc(pool_chain, 1)
            pool.wait_ge(pool_chain, 8)
            pool.affine_select(out=swap[:], in_=swap[:], compare_op=ALU.not_equal, fill=1.0, base=-WAVES,
                               pattern=[[-1, P]], channel_multiplier=1).then_inc(pool_chain, 1)
            pool.memset(zeros[:], 0.0).then_inc(pool_chain, 1)
            pool.memset(ones[:], 1.0).then_inc(pool_chain, 1)
            pool.memset(before[:, 0:1], -3.0e38).then_inc(pool_chain, 1)
            pool.wait_ge(pool_chain, 12)
            pool.engine_nop().then_inc(consts_set, 1)

            def multiply_ramp(g):
                cols = slice(g * HG, g * HG + HG) if isinstance(g, int) else bass.ds(g * HG, HG)
                if later(g, 1):
                    pool.wait_ge(k_summed, g)
                    pool.wait_ge(wave_set, g)
                for rates_of, table, done in ((decay, wave, damp_arg_set), (turns, phase, phase_set)):
                    if isinstance(g, int) and g == 0:
                        pool.wait_ge(rates_set if table is wave else turns_set, 1)
                    for s in range(2):
                        ins = pool.tensor_tensor(table[:, s], bc(rates_of[:, s, cols], 2, [P, HG, STEP]),
                                                 bc(ramp[:], 1, [P, HG, STEP]), ALU.mult)
                    ins.then_inc(done, 1)

            def split_y(t, u):
                pool.wait_ge(y_hi_set, t + 1)
                if later(t, 2):
                    pool.wait_ge(lin_done[1], t - 1)
                pool.tensor_tensor(y_lo[:, u], y[:].rearrange("p i h b -> p i (h b)"), y_hi[:, u].bitcast(F32),
                                   ALU.subtract).then_inc(y_lo_set, 1)

            def add_bias(t, u):
                pool.wait_ge(xr_in[u], uses(t, u))
                pool.tensor_tensor(res[:, u], res[:, u], bias_all[:], ALU.add).then_inc(bias_set, 1)

            multiply_ramp(0)
            for n, k in enumerate((*range(W_POOL), BLOCKS)):
                if k == 2:
                    multiply_ramp(1)
                pool.wait_ge(w_hi_set, k + 1)
                lo, hi = (w_lo[:, k], w_hi[:, k]) if k < BLOCKS else (b_lo[:], b_hi[:])
                pool.tensor_tensor(lo, w_raw[k], hi.bitcast(F32), ALU.subtract).then_inc(w_lo_set, 1)
            pool.wait_ge(bias_in, 16)

            def step(i, t, u):
                if u == 1 and known(i + 2, GROUPS):
                    multiply_ramp(i + 2)
                if known(t, TILES):
                    split_y(t, u)
                    add_bias(t, u)

            run_steps(pool, step)

        @block.scalar
        def _(act):
            def damp_waves(g):
                act.wait_ge(damp_arg_set, g + 1)
                act.activation(wave[:], wave[:], ACT.Exp).then_inc(damp_set, 1)

            def turn_waves(g):
                act.wait_ge(wrapped_set, g + 1)
                act.activation(phase[:], phase[:], ACT.Sin, bias=quarter_rad[:], scale=-TURN).then_inc(trig_set, 1)

            def split_x(t, u):
                act.wait_ge(x_scale_set, t + 1)
                if later(t, 2):
                    act.wait_ge(conv_done, 2 * t - 2)
                act.activation(x_hi[:, u], xc[:, u].rearrange("p h i b -> p h (i b)"), ACT.Copy,
                               scale=x_scale[:, u:u + 1]).then_inc(x_hi_set, 1)

            def split_w(k):
                act.wait_ge(w_in[k // 2], 16)
                act.activation(w_hi[:, k] if k < BLOCKS else b_hi[:], w_raw[k], ACT.Copy).then_inc(w_hi_set, 1)

            def split_y(t, u):
                act.wait_ge(y_set, 2 * t + 2)
                if later(t, 2):
                    act.wait_ge(lin_done[1], t - 1)
                act.activation(y_hi[:, u], y[:].rearrange("p i h b -> p i (h b)"), ACT.Copy).then_inc(y_hi_set, 1)

            def split_z(t):
                act.wait_ge(z_turn_done, t + 1)
                if later(t, 1):
                    act.wait_ge(lin_done[1], t)
                act.activation(z_parts[:], z_turned[:, 0:P], ACT.Copy).then_inc(z_hi_set, 1)

            act.wait_ge(rates_set, 1)
            act.activation(sm["tanh"][:], decay[:, 0], ACT.Tanh, scale=0.5).then_inc(half_set, 1)
            damp_waves(0)
            act.wait_ge(turns_set, 1)
            act.activation(sm["sin"][:], turns[:, 0], ACT.Sin, scale=0.5 * TURN).then_inc(half_set, 1)
            act.activation(sm["cos"][:], turns[:, 0], ACT.Sin, bias=quarter_all[:], scale=0.5 * TURN)\
                .then_inc(half_set, 1)
            split_w(0)
            turn_waves(0)
            for k in range(1, BLOCKS):
                split_w(k)
            split_x(0, 0)
            damp_waves(1)
            turn_waves(1)
            split_x(1, 1)
            split_w(BLOCKS)

            def step(i, t, u):
                if u == 1 and known(i + 2, GROUPS):
                    damp_waves(i + 2)
                if known(t, TILES):
                    split_y(t, u)
                if known(t + 1, TILES) and later(t, 1):
                    split_x(t + 1, 1 - u)
                if later(t, 1):
                    split_z(t - 1)
                if u == 1 and known(i + 2, GROUPS):
                    turn_waves(i + 2)

            run_steps(act, step)

        @block.tensor
        def _(pe):
            def swap_waves(g):
                pe.wait_ge(wave_set, g + 1)
                pe.matmul(z_turned[:, P:P + HG * STEP], swap[:], wave[:, 1], start=True, stop=True)\
                    .then_inc(swap_done, 1)

            def sum_waves(g):
                pe.wait_ge(mode_set, g + 1)
                if later(g, 1):
                    pe.wait_ge(k_split, g)
                for q in range(QUADS):
                    mm = pe.matmul(k_sum[:, q], mode[:, HT * q:HT * q + HT], wave[:, 0, HT * q:HT * q + HT],
                                   start=True, stop=True)
                mm.then_inc(k_summed, 1)

            def sum_tops(t, u):
                pe.wait_ge(x_top_set, t + 1)
                pe.matmul(x_sum[:, u:u + 1], ones[:], x_top[:, u:u + 1], start=True, stop=True).then_inc(x_sum_done, 1)

            def convolve(t, u):
                if later(t, 2):
                    pe.wait_ge(toep_in[u], uses(t, u) - 16)
                for h in range(HT):
                    if isinstance(t, int) and t < 2:
                        pe.wait_ge(early[t][h], 32 - 16 * t)
                    if isinstance(t, int) and t == 0 and h == 2:
                        swap_waves(1)
                    if h % 2 == 0 and later(t, 1):
                        pe.wait_ge(y_set, 2 * t - 1 + h // 2)
                    for d in range(BLOCKS):
                        n = (BLOCKS - d) * BATCH
                        for part, x in ((0, x_hi), (0, x_lo), (1, x_hi)):
                            mm = pe.matmul(conv[h // 2][:, h % 2, d:BLOCKS], toep[:, u, part, h, d * P:(d + 1) * P],
                                           x[:, u, h, 0:n], start=(d == 0 and part == 0 and x is x_hi),
                                           stop=(d == BLOCKS - 1 and part == 1))
                    if h % 2 == 1:
                        mm.then_inc(conv_done, 1)

            def linear(t, u, g=None):
                pe.wait_ge(y_lo_set, t + 1)
                for n, c in enumerate((2, 0, 1)):
                    if later(t, 1):
                        pe.wait_ge(res_set, 3 * t - 2 + n)
                    for k in range(BLOCKS):
                        if isinstance(t, int) and t == 0 and c == 2:
                            if k < W_POOL:
                                pe.wait_ge(w_lo_set, k + 1)
                            else:
                                pe.wait_ge(w_lo_late_set, k - W_POOL + 1)
                        for first, second in ((y_hi, w_hi), (y_hi, w_lo), (y_lo, w_hi)):
                            mm = pe.matmul(lin[c][:, 0:CH], first[:, u, k], second[:, k, c * CH:(c + 1) * CH],
                                           start=(k == 0 and first is y_hi and second is w_hi),
                                           stop=(k == BLOCKS - 1 and first is y_lo))
                    if c == 2:
                        mm.then_inc(z_done, 1)
                    if c == 0:
                        if g is not None:
                            sum_waves(g)
                        pe.wait_ge(z_open_set, t + 1)
                        if later(t, 1):
                            pe.wait_ge(z_lo_set, t)
                        pe.transpose(z_turned[:, 0:P], z_open[:], ident[:]).then_inc(z_turn_done, 1)
                if isinstance(t, int) and t == 0:
                    pe.wait_ge(w_lo_set, W_POOL + 1)
                pe.wait_ge(z_lo_set, t + 1)
                for c in (2, 0, 1):
                    w = Z0 if c == 2 else CH
                    for rows, b in ((P, b_hi), (RMAX, b_lo)):
                        mm = pe.matmul(lin[c][:, 0:w], z_parts[0:rows], b[0:rows, c * CH:c * CH + w],
                                       start=False, stop=True, skip_group_check=True)
                    mm.then_inc(lin_done[c], 1)

            pe.wait_ge(consts_set, 1)
            swap_waves(0)
            pe.wait_ge(sizes_set, 1)
            pe.matmul(k_bound_sum, ones[:], k_sizes[:], start=True, stop=True).then_inc(bound_done, 1)
            sum_waves(0)
            sum_tops(0, 0)
            sum_tops(1, 1)
            for _ in range(WARM_UP):
                pe.matmul(lin[0][:], ones[:], bc(ones[:], 1, [P, 4, P]), start=True, stop=True)

            def step(i, t, u):
                if known(t, TILES):
                    pe.wait_ge(x_lo_set, t + 1)
                    convolve(t, u)
                if isinstance(t, int) and t == 0:
                    sum_waves(1)
                if known(t + 1, TILES) and later(t, 1):
                    sum_tops(t + 1, 1 - u)
                if later(t, 1):
                    linear(t - 1, 1 - u, i + 1 if u == 0 and known(i + 1, GROUPS) else None)

            run_steps(pe, step)

        @block.vector
        def _(dve):
            chained = [0]

            def link(ins):
                ins.then_inc(dve_chain, 1)
                chained[0] += 1
                return chained[0]

            def settle(upto=None):
                dve.wait_ge(dve_chain, upto or chained[0])

            s = {n: v[:] for n, v in sm.items()}
            tt = dve.tensor_tensor

            def stt(o, a, scalar, b, op0, op1):
                return dve.scalar_tensor_tensor(out=o, in0=a, scalar=scalar, in1=b, op0=op0, op1=op1)

            for tile, upper, lower in ((quarter, 0.25, 0.0), (quarter_rad, 0.25 * TURN, 0.0), (twice_sign, 2.0, -2.0)):
                link(dve.memset(tile[0:WAVES], upper))
                link(dve.memset(tile[WAVES:P], lower))
            link(dve.memset(quarter_all[:], 0.25 * TURN))
            dve.wait_ge(rates_in, 16)
            arg, ai, cre, cim = rate[:, 0:2], rate[:, 2], coef[:, 0], coef[:, 1]
            n = link(dve.tensor_scalar(ex["k"][:], arg, LOG2E, MAGIC, ALU.mult, ALU.add))
            link(tt(s["ai2"], ai, ai, ALU.mult))
            settle(n)
            n = link(dve.tensor_scalar(ex["k"][:], ex["k"][:], MAGIC, None, ALU.subtract))
            link(stt(s["abs_skip"], rate[:, 3], -1.0, rate[:, 3], ALU.mult, ALU.max))
            settle(n)
            n = link(stt(ex["r"][:], ex["k"][:], -LN2_HI, arg, ALU.mult, ALU.add))
            dve.wait_ge(coefs_in, 16)
            link(tt(s["cim_ai"], cim, ai, ALU.mult))
            settle(n)
            link(stt(ex["r"][:], ex["k"][:], -LN2_LO, ex["r"][:], ALU.mult, ALU.add))
            n = link(dve.tensor_scalar(ex["k"][:], ex["k"][:], 126.0, -126.0, ALU.min, ALU.max))
            link(tt(s["cre_ai"], cre, ai, ALU.mult))
            settle(n)
            n = link(dve.tensor_scalar(ex["p"][:], ex["r"][:], 1.0 / math.factorial(7), None, ALU.mult))
            link(dve.tensor_scalar(ex_bits[:], ex["k"][:], 127.0, float(1 << 23), ALU.add, ALU.mult))
            for f in range(6, 0, -1):
                settle(n)
                n = link(stt(ex["p"][:], ex["p"][:], 1.0 / math.factorial(f), ex["r"][:], ALU.add, ALU.mult))
            settle()
            link(stt(ex["e"][:], ex["p"][:], 1.0, ex_bits[:].bitcast(F32), ALU.add, ALU.mult))
            settle()
            dt, ar = ex["e"][:, 0], ex["e"][:, 1]
            n = link(stt(decay[:, 0], ar, -1.0, dt, ALU.mult, ALU.mult))
            m = link(tt(theta[:, 0], ai, dt, ALU.mult))
            settle(n)
            dve.tensor_scalar(decay[:, 1], decay[:, 0], float(STEP), None, ALU.mult).then_inc(rates_set, 1)
            settle(m)
            n = link(dve.tensor_scalar(theta[:, 1], theta[:, 0], float(STEP), None, ALU.mult))
            link(tt(s["ar2"], ar, ar, ALU.mult))
            settle(n)
            n = link(dve.tensor_scalar(th_k[:], theta[:], 1.0 / (2 * math.pi), MAGIC, ALU.mult, ALU.add))
            link(tt(s["cre_ar"], cre, ar, ALU.mult))
            settle(n)
            n = link(dve.tensor_scalar(th_k[:], th_k[:], MAGIC, None, ALU.subtract))
            link(tt(s["cim_ar"], cim, ar, ALU.mult))
            for part, between in (
                    (PI2_HI, (s["rabs2"], s["ar2"], s["ai2"], ALU.add)),
                    (PI2_MID, (s["qre"], s["cim_ai"], s["cre_ar"], ALU.subtract)),
                    (PI2_LO, (s["qim"], s["cre_ai"], s["cim_ar"], ALU.add))):
                settle(n)
                n = link(stt(theta[:], th_k[:], -part, theta[:], ALU.mult, ALU.add))
                link(tt(*between))
            settle()
            dve.tensor_scalar(turns[:], theta[:], 1.0 / (2 * math.pi), None, ALU.mult).then_inc(turns_set, 1)
            link(dve.reciprocal(s["rabs2"], s["rabs2"]))
            settle()
            link(tt(s["qre"], s["qre"], s["rabs2"], ALU.mult))
            link(tt(s["qim"], s["qim"], s["rabs2"], ALU.mult))
            dve.wait_ge(turns_set, 1)
            dve.wait_ge(consts_set, 1)

            def wrap_phases(g):
                dve.wait_ge(phase_set, g + 1)
                if later(g, 1):
                    dve.wait_ge(wrapped_set, g)
                dve.tensor_scalar(whole[:], phase[:], quarter[:], MAGIC, ALU.add, ALU.add).then_inc(whole_set, 1)
                dve.wait_ge(whole_set, g + 1)
                dve.scalar_tensor_tensor(out=phase[:], in0=whole[:], scalar=MAGIC, in1=phase[:],
                                         op0=ALU.subtract, op1=ALU.subtract).then_inc(wrapped_set, 1)

            def finish_waves(g):
                dve.wait_ge(damp_set, g + 1)
                dve.wait_ge(trig_set, g + 1)
                dve.tensor_tensor(wave[:], wave[:], phase[:], ALU.mult).then_inc(wave_set, 1)

            def weigh_waves(g):
                cols = slice(g * HG, g * HG + HG) if isinstance(g, int) else bass.ds(g * HG, HG)
                dve.wait_ge(wave_set, g + 1)
                if later(g, 1):
                    dve.wait_ge(k_summed, g)
                tt(mode_re[:], wave[:, 1], bc(sm["gre"][:, cols], 2, [P, HG, STEP]), ALU.mult).then_inc(mode_chain, 1)
                if later(g, 2):
                    dve.wait_ge(swap_in, 32 * g - 32)
                    swapped = swapped_sb[:]
                else:
                    dve.wait_ge(swap_done, g + 1)
                    swapped = swapped_early
                tt(mode_im[:], swapped, bc(sm["gim"][:, cols], 2, [P, HG, STEP]), ALU.mult).then_inc(mode_chain, 1)
                dve.wait_ge(mode_chain, 2 * g + 2)
                tt(mode[:], mode_re[:], mode_im[:], ALU.add).then_inc(mode_set, 1)

            def take_kernels(g):
                dve.wait_ge(k_summed, g + 1)
                if later(g, 1):
                    dve.wait_ge(k_split, g)
                if later(g, 2):
                    dve.wait_ge(k_out, (g - 1) * (16 * HT))
                quads = slice(g * QUADS, g * QUADS + QUADS) if isinstance(g, int) else bass.ds(g * QUADS, QUADS)
                for j in range(HT):
                    rows = slice(STEP * j, STEP * (j + 1))
                    tt(kern[rows], k_sum[rows, :, j], bc(k_scale[rows, quads], 2, [STEP, QUADS, STEP]), ALU.mult)\
                        .then_inc(kern_chain, 1)
                dve.wait_ge(kern_chain, 6 * g + 4)
                tt(kern[:, :, 0], kern[:, :, 0], skip_q[:, quads], ALU.add).then_inc(kern_chain, 1)
                dve.wait_ge(kern_chain, 6 * g + 5)
                dve.tensor_copy(k_parts[:, :, 0], kern[:]).then_inc(kern_chain, 1)
                dve.wait_ge(kern_chain, 6 * g + 6)
                tt(k_parts[:, :, 1], kern[:], k_parts[:, :, 0], ALU.subtract).then_inc(k_split, 1)

            def top_x(t, u):
                dve.wait_ge(xc_in[u], uses(t, u))
                dve.tensor_reduce(x_top[:, u:u + 1], xc[:, u].rearrange("p h i b -> p (h i b)"), AX.X, ALU.max,
                                  apply_absolute_value=True).then_inc(x_top_set, 1)

            def scale_x(t, u):
                dve.wait_ge(x_sum_done, t + 1)
                dve.tensor_scalar(x_pow[:, u:u + 1], x_sum[:, u:u + 1], 2.0**-60, None, ALU.max).then_inc(x_chain, 1)
                dve.wait_ge(x_chain, 3 * t + 1)
                dve.tensor_scalar(x_pow[:, u:u + 1].bitcast(I32), x_pow[:, u:u + 1].bitcast(I32), EXPONENT_BITS, None,
                                  ALU.bitwise_and).then_inc(x_chain, 1)
                dve.wait_ge(x_chain, 3 * t + 2)
                dve.reciprocal(x_rec[:, u:u + 1], x_pow[:, u:u + 1]).then_inc(x_chain, 1)
                dve.wait_ge(x_chain, 3 * t + 3)
                dve.tensor_scalar(x_scale[:, u:u + 1], x_rec[:, u:u + 1], 2.0**14, None, ALU.mult)\
                    .then_inc(x_scale_set, 1)

            def split_x(t, u):
                dve.wait_ge(x_hi_set, t + 1)
                dve.scalar_tensor_tensor(
                    out=x_lo[:, u].rearrange("p h n -> p (h n)"), in0=xc[:, u].rearrange("p h i b -> p (h i b)"),
                    scalar=x_scale[:, u:u + 1], in1=x_hi[:, u].rearrange("p h n -> p (h n)"), op0=ALU.mult,
                    op1=ALU.subtract).then_inc(x_lo_set, 1)

            def split_w(k):
                dve.wait_ge(w_hi_set, k + 1)
                tt(w_lo[:, k], w_raw[k], w_hi[:, k].bitcast(F32), ALU.subtract).then_inc(w_lo_late_set, 1)

            wrap_phases(0)
            dve.wait_ge(half_set, 3)
            n = link(dve.tensor_scalar(s["den"], s["tanh"], -1.0, 1.0, ALU.mult, ALU.add))
            link(tt(s["n1"], s["sin"], s["sin"], ALU.mult))
            link(tt(s["n2"], s["sin"], s["cos"], ALU.mult))
            settle(n)
            link(dve.reciprocal(s["den"], s["den"]))
            settle()
            link(stt(s["em"], s["tanh"], 2.0, s["den"], ALU.mult, ALU.mult))
            finish_waves(0)
            settle()
            n = link(stt(s["n3"], s["em"], 1.0, s["n1"], ALU.add, ALU.mult))
            m = link(stt(s["n4"], s["em"], 1.0, s["n2"], ALU.add, ALU.mult))
            settle(n)
            link(stt(s["zre"], s["n3"], -2.0, s["em"], ALU.mult, ALU.add))
            settle(m)
            link(dve.tensor_scalar(s["zim"], s["n4"], 2.0, None, ALU.mult))
            settle()
            link(stt(s["n1"], s["qre"], twice_sign[:], s["zre"], ALU.mult, ALU.mult))
            n = link(stt(s["n2"], s["qim"], twice_sign[:], s["zim"], ALU.mult, ALU.mult))
            link(stt(s["n3"], s["qim"], 2.0, s["zre"], ALU.mult, ALU.mult))
            m = link(stt(s["n4"], s["qre"], 2.0, s["zim"], ALU.mult, ALU.mult))
            settle(n)
            link(tt(s["gre"], s["n1"], s["n2"], ALU.add))
            settle(m)
            link(tt(s["gim"], s["n3"], s["n4"], ALU.subtract))
            settle()
            link(stt(s["n1"], s["gre"], -1.0, s["gre"], ALU.mult, ALU.max))
            link(stt(s["n2"], s["gim"], -1.0, s["gim"], ALU.mult, ALU.max))
            settle()
            tt(k_sizes[:], s["n1"], s["n2"], ALU.add).then_inc(sizes_set, 1)
            weigh_waves(0)
            dve.wait_ge(bound_done, 1)
            link(stt(k_bound[:], k_bound_sum, 2.0**-60, s["abs_skip"], ALU.max, ALU.add))
            settle()
            link(dve.tensor_reduce(k_pow[:], k_bound[:].rearrange("p (t h) -> p t h", h=HT), AX.X, ALU.max))
            settle()
            link(dve.tensor_scalar(k_pow[:].bitcast(I32), k_pow[:].bitcast(I32), EXPONENT_BITS, None, ALU.bitwise_and))
            settle()
            link(dve.reciprocal(k_scale[:], k_pow[:]))
            settle()
            link(dve.tensor_scalar(k_scale[:], k_scale[:], 2.0**14, None, ALU.mult))
            settle()
            dve.wait_ge(skip_in, 16 * HT)
            link(tt(skip_q[:], skip_q[:], k_scale[:], ALU.mult))
            settle()
            take_kernels(0)
            top_x(0, 0)
            top_x(1, 1)
            dve.wait_ge(x_sum_done, 2)
            scale_x(0, 0)
            wrap_phases(1)
            split_x(0, 0)
            scale_x(1, 1)

            dve.wait_ge(len_in, 16)
            link(dve.tensor_copy(len_f[:], len_i[:]))
            settle()
            link(tt(mask[:], bc(pos_f[:], 2, [P, BLOCKS, BATCH]), bc(len_f[:], 1, [P, BLOCKS, BATCH]), ALU.is_lt))
            settle()
            split_w(6)
            finish_waves(1)
            split_w(7)
            weigh_waves(1)
            split_x(1, 1)
            dve.wait_ge(gate_in, 16)

            def take_y(t, u, n):
                if n == 0:
                    stt(unscale[:, u:u + 1], x_pow[:, u:u + 1], 2.0**-28, k_pow[:, bass.ds(t, 1)], ALU.mult, ALU.mult)\
                        .then_inc(unscale_set, 1)
                    dve.wait_ge(unscale_set, t + 1)
                    if later(t, 1):
                        dve.wait_ge(y_lo_set, t)
                dve.wait_ge(conv_done, 2 * t + n + 1)
                for h in range(2):
                    ins = stt(y[:, :, 2 * n + h], conv[n][:, h], unscale[:, u:u + 1], mask[:], ALU.mult, ALU.mult)
                ins.then_inc(y_set, 1)

            def pick_rank(t):
                z = lin[2][:, Z0:Z0 + RMAX]
                dve.wait_ge(z_done, t + 1)
                tt(score[:], lin[2][:, Z0 + RMAX:Z0 + RMAX + 4], gate_bias[:], ALU.add).then_inc(gate_chain, 1)
                dve.wait_ge(gate_chain, 4 * t + 1)
                dve.tensor_reduce(best[:], score[:], AX.X, ALU.max)
                dve.tensor_copy(before[:, 1:2], score[:, 0:1])
                tt(before[:, 2:4], score[:, 0:1].broadcast_to([P, 2]), score[:, 1:2].broadcast_to([P, 2]), ALU.max)\
                    .then_inc(gate_chain, 1)
                dve.wait_ge(gate_chain, 4 * t + 2)
                tt(before[:, 4:8], before[:, 2:3].broadcast_to([P, 4]), score[:, 2:3].broadcast_to([P, 4]), ALU.max)\
                    .then_inc(gate_chain, 1)
                dve.wait_ge(gate_chain, 4 * t + 3)
                dve.tensor_scalar(open8[:], before[:], best[:], None, ALU.is_lt).then_inc(gate_chain, 1)
                dve.wait_ge(gate_chain, 4 * t + 4)
                if later(t, 1):
                    dve.wait_ge(z_turn_done, t)
                for twice in range(2):
                    ins = tt(z_open[:, twice].rearrange("p (g c) -> p g c", g=8), z.rearrange("p (g c) -> p g c", g=8),
                             bc(open8[:], 2, [P, 8, 8]), ALU.mult)
                ins.then_inc(z_open_set, 1)

            def split_z(t):
                dve.wait_ge(z_hi_set, t + 1)
                tt(z_parts[RMAX:P], z_turned[RMAX:P, 0:P], z_parts[RMAX:P].bitcast(F32), ALU.subtract)\
                    .then_inc(z_lo_set, 1)

            def finish(t, u):
                dve.wait_ge(bias_set, t + 1)
                for c in (2, 0, 1):
                    w = Z0 if c == 2 else CH
                    dve.wait_ge(lin_done[c], t + 1)
                    tt(res[:, u, c * CH:c * CH + w], res[:, u, c * CH:c * CH + w], lin[c][:, 0:w], ALU.add)\
                        .then_inc(res_set, 1)

            def step(i, t, u):
                if known(t + 1, TILES) and later(t, 1):
                    top_x(t + 1, 1 - u)
                if known(t, TILES):
                    take_y(t, u, 0)
                    take_y(t, u, 1)
                if isinstance(t, int) and t == 0:
                    take_kernels(1)
                if known(t + 1, TILES) and later(t, 1):
                    scale_x(t + 1, 1 - u)
                if u == 0 and known(i + 1, GROUPS) and later(t, 1):
                    weigh_waves(i + 1)
                if later(t, 1):
                    pick_rank(t - 1)
                if u == 1 and known(i + 2, GROUPS):
                    wrap_phases(i + 2)
                if known(t + 1, TILES) and later(t, 1):
                    split_x(t + 1, 1 - u)
                if u == 0 and known(i + 1, GROUPS) and later(t, 1):
                    take_kernels(i + 1)
                if later(t, 1):
                    split_z(t - 1)
                    finish(t - 1, 1 - u)
                if u == 1 and known(i + 2, GROUPS):
                    finish_waves(i + 2)

            run_steps(dve, step)


def kernel(x, itok_B_8_3872, L0_cond_log_dt, L0_cond_C, L0_cond_log_A_real, L0_cond_A_imag, L0_cond_D,
           L0_ffn_W, L0_ffn_b, L0_ffn_A, L0_ffn_B, L0_ffn_gate_w, L0_ffn_gate_b):
    import concourse.bacc as bacc
    from concourse.bass_utils import run_bass_kernel_spmd

    def lay(a):
        return np.ascontiguousarray(a)

    x = np.asarray(x)
    x_rows = lay(x.transpose(1, 0, 2).reshape(TILES, P, LENGTH))
    x_cols = lay(x.reshape(BATCH, TILES, HT, BLOCKS, P)[..., ::-1].transpose(1, 4, 2, 3, 0))
    twice = lambda a: np.concatenate([a, a])
    log_dt = np.broadcast_to(np.asarray(L0_cond_log_dt), (WAVES, FEATURES))
    all_skip = np.broadcast_to(np.asarray(L0_cond_D), (WAVES, FEATURES))
    rates = lay(twice(np.stack([log_dt, np.asarray(L0_cond_log_A_real).T, np.asarray(L0_cond_A_imag).T, all_skip], 1)))
    coefs = lay(twice(np.asarray(L0_cond_C).transpose(1, 2, 0)))
    skip = lay(np.asarray(L0_cond_D).reshape(TILES, HT).T)
    weights = lay(np.concatenate([np.asarray(a) for a in (L0_ffn_W, L0_ffn_A, L0_ffn_gate_w)]).T
                  .reshape(BLOCKS, P, COLS))
    lora_b = lay(twice(np.asarray(L0_ffn_B).T))

    nc = bacc.Bacc("TRN2", target_bir_lowering=False, num_devices=1)
    arrays = {
        "x_rows": x_rows, "x_cols": x_cols, "lengths": lay(itok_B_8_3872), "rates": rates, "coefs": coefs,
        "skip": skip, "weights": weights, "bias": lay(L0_ffn_b), "lora_b": lora_b, "gate_b": lay(L0_ffn_gate_b),
    }
    args = [nc.dram_tensor(n, a.shape, mybir.dt.from_np(a.dtype), kind="ExternalInput").ap() for n, a in arrays.items()]
    scratch = nc.dram_tensor("kernels", (TILES, 2, HT, KROW), F16, kind="Internal").ap()
    out = nc.dram_tensor("out", (TILES, P, LENGTH), F32, kind="ExternalOutput").ap()
    build(nc, *args, scratch, out)
    r = run_bass_kernel_spmd(nc, [arrays], core_ids=[0])
    return r.results[0]["out"].reshape(FEATURES, BATCH, LENGTH).transpose(1, 0, 2)
```
